# Optimizing a Trainium2 kernel written in Bass

```python
import numpy as np
import jax
import jax.numpy as jnp

def _softmax(x, axis=-1):
    return jax.nn.softmax(x, axis=axis)

def _gelu(x):
    return jax.nn.gelu(x, approximate=True)

def _silu(x):
    return jax.nn.silu(x)

def _sigmoid(x):
    return jax.nn.sigmoid(x)

def _layernorm(x, axis=-1, eps=1e-05):
    m = jnp.mean(x, axis=axis, keepdims=True)
    v = jnp.var(x, axis=axis, keepdims=True)
    return (x - m) / jnp.sqrt(v + eps)

def _scatter_add(tgt, idx, src, axis=0):
    return tgt.at[idx].add(src)

def _segment_sum(src, seg, n):
    return jax.ops.segment_sum(src, seg, n)
kernel_name = 'mk_conv_preact_d4_conv_nchw16_r4_534e66'

def setup_inputs(seed: int=0):
    np.random.seed(seed)
    _w = jnp.asarray

    def _rec_inputs():
        import jax
        import jax.numpy as jnp
        _gk = jax.random.key(seed)
        x = -0.0005207 + 1.001 * jax.random.normal(jax.random.fold_in(_gk, 1), (8, 16, 32, 32), jnp.float32)
        return x
    x = _rec_inputs()

    def _L0_conv_setup():
        import jax, jax.numpy as jnp
        import numpy as np
        from jax import lax
        NUM_COLS = 4
        NUM_ROWS = 4
        C = 16
        K = 3
        B, H, Wd = (8, 32, 32)
        W_SCALE = 0.05

        def _cell(w, bias, ins):
            if len(ins) < 3:
                pad_shape = (ins[0].shape[0], (3 - len(ins)) * C) + ins[0].shape[2:]
                ins = ins + [jnp.zeros(pad_shape, dtype=ins[0].dtype)]
            x = jnp.concatenate(ins, axis=1)
            y = lax.conv_general_dilated(x, w, window_strides=(1, 1), padding='SAME', dimension_numbers=('NCHW', 'OIHW', 'NCHW'))
            y = jax.nn.relu(y + bias[None, :, None, None])
            right, up, down = jnp.split(y, 3, axis=1)
            return (right, up, down)
        key = jax.random.key(seed)
        k1, k2 = jax.random.split(key, 2)
        x = jax.random.normal(k1, (B, C, H, Wd), dtype=jnp.float32)
        W = jax.random.normal(k2, (NUM_COLS, NUM_ROWS, 3 * C, 3 * C, K, K), dtype=jnp.float32) * W_SCALE
        b = jnp.zeros((NUM_COLS, NUM_ROWS, 3 * C), dtype=jnp.float32)
        return {'input_tensor': x, 'W': W, 'b': b}
    _L0_conv_all = _L0_conv_setup()
    _L0_conv_in = {k: v for k, v in _L0_conv_all.items() if k in ('W', 'b')}
    del _L0_conv_all

    def _L1_conv_setup():
        import jax, jax.numpy as jnp
        import numpy as np
        KERNEL_SIZE = 3
        STRIDE = 1
        PADDING = 1
        key = jax.random.key(seed)
        k1, k2 = jax.random.split(key)
        x = jax.random.normal(k1, (16, 16, 128, 128), dtype=jnp.float32)
        K = jax.random.normal(k2, (3, 3, 16, 16), dtype=jnp.float32)
        return {'x': x, 'K': K}
    _L1_conv_all = _L1_conv_setup()
    _L1_conv_in = {k: v for k, v in _L1_conv_all.items() if k in ('K',)}
    del _L1_conv_all

    def _L2_conv_setup():
        import jax, jax.numpy as jnp
        import numpy as np
        key = jax.random.key(seed)
        uvs = jax.random.normal(key, (16, 16, 128, 64), dtype=jnp.float32)
        return {'uvs': uvs}
    _L2_conv_all = _L2_conv_setup()
    _L2_conv_in = {k: v for k, v in _L2_conv_all.items() if k in ()}
    del _L2_conv_all

    def _L3_conv_setup():
        import jax, jax.numpy as jnp
        import numpy as np
        from jax import lax
        NUM_COLS = 4
        NUM_ROWS = 4
        C = 16
        K = 3
        B, H, Wd = (8, 32, 32)
        W_SCALE = 0.05

        def _cell(w, bias, ins):
            if len(ins) < 3:
                pad_shape = (ins[0].shape[0], (3 - len(ins)) * C) + ins[0].shape[2:]
                ins = ins + [jnp.zeros(pad_shape, dtype=ins[0].dtype)]
            x = jnp.concatenate(ins, axis=1)
            y = lax.conv_general_dilated(x, w, window_strides=(1, 1), padding='SAME', dimension_numbers=('NCHW', 'OIHW', 'NCHW'))
            y = jax.nn.relu(y + bias[None, :, None, None])
            right, up, down = jnp.split(y, 3, axis=1)
            return (right, up, down)
        key = jax.random.key(seed)
        k1, k2 = jax.random.split(key, 2)
        x = jax.random.normal(k1, (B, C, H, Wd), dtype=jnp.float32)
        W = jax.random.normal(k2, (NUM_COLS, NUM_ROWS, 3 * C, 3 * C, K, K), dtype=jnp.float32) * W_SCALE
        b = jnp.zeros((NUM_COLS, NUM_ROWS, 3 * C), dtype=jnp.float32)
        return {'input_tensor': x, 'W': W, 'b': b}
    _L3_conv_all = _L3_conv_setup()
    _L3_conv_in = {k: v for k, v in _L3_conv_all.items() if k in ('W', 'b')}
    del _L3_conv_all
    return {'x': x, 'L0_conv_W': _L0_conv_in['W'], 'L0_conv_b': _L0_conv_in['b'], 'L1_conv_K': _L1_conv_in['K'], 'L3_conv_W': _L3_conv_in['W'], 'L3_conv_b': _L3_conv_in['b']}

def reference(x, L0_conv_W, L0_conv_b, L1_conv_K, L3_conv_W, L3_conv_b):
    import jax
    import jax.numpy as jnp

    def _L0_conv_ref(input_tensor, W, b):
        import jax, jax.numpy as jnp
        import numpy as np
        from jax import lax
        NUM_COLS = 4
        NUM_ROWS = 4
        C = 16
        K = 3
        B, H, Wd = (8, 32, 32)
        W_SCALE = 0.05

        def _cell(w, bias, ins):
            if len(ins) < 3:
                pad_shape = (ins[0].shape[0], (3 - len(ins)) * C) + ins[0].shape[2:]
                ins = ins + [jnp.zeros(pad_shape, dtype=ins[0].dtype)]
            x = jnp.concatenate(ins, axis=1)
            y = lax.conv_general_dilated(x, w, window_strides=(1, 1), padding='SAME', dimension_numbers=('NCHW', 'OIHW', 'NCHW'))
            y = jax.nn.relu(y + bias[None, :, None, None])
            right, up, down = jnp.split(y, 3, axis=1)
            return (right, up, down)
        outs = [None] * NUM_ROWS
        for col in range(NUM_COLS):
            for row in range(NUM_ROWS):
                if col == 0:
                    ins = [input_tensor] if row == 0 else [outs[row - 1][-1]]
                elif row == 0:
                    ins = [outs[row][0], outs[row + 1][1]]
                elif row == NUM_ROWS - 1:
                    ins = [outs[row][0], outs[row - 1][-1]]
                else:
                    ins = [outs[row][0], outs[row + 1][1], outs[row - 1][-1]]
                outs[row] = _cell(W[col, row], b[col, row], ins)
        return outs[-1][0]

    def _L1_conv_ref(x, K):
        import jax, jax.numpy as jnp
        import numpy as np
        KERNEL_SIZE = 3
        STRIDE = 1
        PADDING = 1
        k = KERNEL_SIZE
        C = x.shape[1]
        O = K.shape[-1]
        Kw = K.reshape(k * k * C, O).reshape(C, k, k, O)
        Kw = jnp.transpose(Kw, (1, 2, 0, 3))
        y = jax.lax.conv_general_dilated(x, Kw, window_strides=(STRIDE, STRIDE), padding=[(PADDING, PADDING), (PADDING, PADDING)], dimension_numbers=('NCHW', 'HWIO', 'NCHW'))
        P = x.shape[-1] + 2 * PADDING
        n_loop = len(range(0, P - k, STRIDE))
        out_size = (P - k) // STRIDE + 1
        idx = jnp.arange(out_size)
        m = (idx < n_loop).astype(y.dtype)
        y = y * m[:, None] * m[None, :]
        return y

    def _L2_conv_ref(uvs):
        import jax, jax.numpy as jnp
        import numpy as np
        u, v = jnp.split(uvs, 2, axis=1)
        left_gate = jax.nn.relu(jnp.sign(jnp.einsum('bkmd,bkd->bkm', u, v.sum(axis=2))))[..., None]
        right_gate = jax.nn.relu(jnp.sign(jnp.einsum('bknd,bkd->bkn', v, u.sum(axis=2))))[..., None]
        return jnp.concatenate([left_gate * u, right_gate * v], axis=1)

    def _L3_conv_ref(input_tensor, W, b):
        import jax, jax.numpy as jnp
        import numpy as np
        from jax import lax
        NUM_COLS = 4
        NUM_ROWS = 4
        C = 16
        K = 3
        B, H, Wd = (8, 32, 32)
        W_SCALE = 0.05

        def _cell(w, bias, ins):
            if len(ins) < 3:
                pad_shape = (ins[0].shape[0], (3 - len(ins)) * C) + ins[0].shape[2:]
                ins = ins + [jnp.zeros(pad_shape, dtype=ins[0].dtype)]
            x = jnp.concatenate(ins, axis=1)
            y = lax.conv_general_dilated(x, w, window_strides=(1, 1), padding='SAME', dimension_numbers=('NCHW', 'OIHW', 'NCHW'))
            y = jax.nn.relu(y + bias[None, :, None, None])
            right, up, down = jnp.split(y, 3, axis=1)
            return (right, up, down)
        outs = [None] * NUM_ROWS
        for col in range(NUM_COLS):
            for row in range(NUM_ROWS):
                if col == 0:
                    ins = [input_tensor] if row == 0 else [outs[row - 1][-1]]
                elif row == 0:
                    ins = [outs[row][0], outs[row + 1][1]]
                elif row == NUM_ROWS - 1:
                    ins = [outs[row][0], outs[row - 1][-1]]
                else:
                    ins = [outs[row][0], outs[row + 1][1], outs[row - 1][-1]]
                outs[row] = _cell(W[col, row], b[col, row], ins)
        return outs[-1][0]

    def _gn(v, G=8, eps=1e-05):
        B_, C_, H_, W_ = v.shape
        g = v.reshape(B_, G, C_ // G, H_, W_)
        m = jnp.mean(g, axis=(2, 3, 4), keepdims=True)
        s = jnp.var(g, axis=(2, 3, 4), keepdims=True)
        return ((g - m) / jnp.sqrt(s + eps)).reshape(v.shape)

    def _ln_c(v, eps=1e-06):
        m = jnp.mean(v, axis=1, keepdims=True)
        s = jnp.var(v, axis=1, keepdims=True)
        return (v - m) / jnp.sqrt(s + eps)

    def _ln_t(v, eps=1e-05):
        m = jnp.mean(v, axis=-1, keepdims=True)
        s = jnp.var(v, axis=-1, keepdims=True)
        return (v - m) / jnp.sqrt(s + eps)

    def _to_tokens(v):
        B_, C_, H_, W_ = v.shape
        return v.reshape(B_, C_, H_ * W_).transpose(0, 2, 1)

    def _from_tokens(t, like):
        B_, C_, H_, W_ = like.shape
        return t.transpose(0, 2, 1).reshape(B_, C_, H_, W_)
    x = x + _L0_conv_ref(_gn(x), L0_conv_W, L0_conv_b)
    x = x + _L1_conv_ref(_gn(x), L1_conv_K)
    x = x + _L2_conv_ref(_gn(x))
    x = x + _L3_conv_ref(_gn(x), L3_conv_W, L3_conv_b)
    return x

_drawn_inputs = setup_inputs


def setup_inputs(seed=0):
    import zlib

    import numpy as np

    out = dict(_drawn_inputs(seed))
    spreads = {'L0_conv_b': (0.0, 0.1), 'L3_conv_b': (0.0, 0.1)}
    factors = {}
    for name, (base, spread) in spreads.items():
        noise = np.random.default_rng([zlib.crc32(name.encode()), seed]).standard_normal(out[name].shape)
        drawn = base * np.exp(spread * noise) if base else spread * noise
        out[name] = jnp.asarray(drawn.astype(out[name].dtype))
    for name, factor in factors.items():
        out[name] = (out[name] * factor).astype(out[name].dtype)
    return out
```

```python
from contextlib import ExitStack

import numpy as np

import concourse.bass as bass
from concourse import mybir

F32 = mybir.dt.float32
F16 = mybir.dt.float16
ALU = mybir.AluOpType
ACT = mybir.ActivationFunctionType
AX = mybir.AxisListType

COLS, ROWS = 4, 4
N_GRID = COLS * ROWS
C = 16
RIGHT, UP, DOWN = range(3)
IMAGES, SIDE = 8, 32
HALVES = 2
NI = IMAGES // HALVES
PAIRS = SIDE // 2
PITCH = SIDE + 2
STORED = PAIRS + 1
PIX = PAIRS * SIDE
Q = 2 * C
TAPS = 6
W_SCALE = 256.0
GN_EPS = 1e-05
BANKS = 8
T_RING = 4
W_RING = 4
RAW_RING = 3

ORDER = sorted(((c, r) for c in range(COLS) for r in range(ROWS)), key=lambda cr: (2 * cr[0] + cr[1], cr[0]))


def streams_in(c, r):
    if c == 0:
        return [DOWN]
    return [RIGHT] + [UP] * (r < ROWS - 1) + [DOWN] * (r > 0)


def streams_out(c, r):
    if c == COLS - 1:
        return [RIGHT] if r == ROWS - 1 else [DOWN]
    return [RIGHT] + [UP] * (r > 0) + [DOWN] * (r < ROWS - 1)


def target(c, r, stream):
    return {RIGHT: (c + 1, r), UP: (c + 1, r - 1), DOWN: (c, r + 1)}[stream]


def places(c, r, stream):
    ins = streams_in(c, r)
    i = ins.index(stream)
    if len(ins) == 1:
        return [(0, 0, 0), (1, 1, 0), (0, 2, 0)]
    if len(ins) == 2:
        return [(0, i, 0), (1, 2 + i, 0)]
    return [(0, i, 0), (1, i, 1)]


WEIGHT_ROWS = {1: 3 * Q, 2: 4 * Q, 3: 3 * Q}
PASSES = {
    1: [(3 * Q, 0, 0)],
    2: [(4 * Q, 0, 0), (2 * Q, 0, 1)],
    3: [(3 * Q, 0, 0), (3 * Q, 1, 0), (3 * Q, 0, 1)],
}
TILES = {1: 4, 2: 2, 3: 1}

CONV = (-1, -1)
SETS = [("L0", c, r) for c, r in ORDER] + [("L1",) + CONV] + [("L3", c, r) for c, r in ORDER]


def set_shape(s):
    if s[0] == "L1":
        return 1, 1
    return len(streams_in(*s[1:])), len(streams_out(*s[1:]))


def banks_of(n_out):
    return NI // TILES[n_out]


def build(nc, x, weights, biases, consts, out):
    with ExitStack() as ctx:
        def sb(name, shape, dt):
            return ctx.enter_context(nc.sbuf_tensor(name, shape, dt))

        def sem(name):
            return ctx.enter_context(nc.semaphore(name))

        res = sb("res", [128, HALVES, PIX], F32)
        inp = [[sb(f"inp{b}{r}", [128, NI, 2, STORED, PITCH], F16) for r in range(ROWS)] for b in range(HALVES)]
        cell_out = [[sb(f"cell_out{b}{k}", [128, NI, 2, PAIRS, PITCH], F16) for k in range(2)] for b in range(HALVES)]
        normed16 = [sb(f"normed16_{b}", [128, 2, STORED, PITCH], F16) for b in range(HALVES)]
        normed = [sb(f"normed{b}", [128, PIX], F32) for b in range(HALVES)]
        act_out = sb("act_out", [128, T_RING, PIX], F32)
        raw = sb("raw", [128, RAW_RING, TAPS * 3 * Q], F32)
        w16 = sb("w16", [128, W_RING, 2, TAPS * 3 * Q], F16)
        bias = sb("bias", [128, 2 * COLS * ROWS], F32)
        const = sb("const", [128, 257], F32)
        averager, partner, row_mask = const[:, 0:128], const[:, 128:256], const[:, 256:257]
        stat6 = sb("stat6", [128, HALVES, 6], F32)
        stat = sb("stat", [128, HALVES, 16], F32)
        rowsum = sb("rowsum", [128, HALVES, SIDE], F32)
        prod = sb("prod", [128, HALVES, PIX], F32)
        gate = sb("gate", [128, HALVES, PAIRS], F32)
        bank = [ctx.enter_context(nc.psum_tensor(f"bank{i}", [128, PIX], F32)) for i in range(BANKS)]

        x_loaded = [sem(f"x_loaded{b}") for b in range(HALVES)]
        consts_loaded = sem("consts_loaded")
        raw_loaded = [sem(f"raw_loaded{i}") for i in range(RAW_RING)]
        raw_scaled = sem("raw_scaled")
        raw_high = sem("raw_high")
        weights_ready = sem("weights_ready")
        zeroed = sem("zeroed")
        sums_ready = sem("sums_ready")
        act_bank_read = sem("act_bank_read")
        dve_bank_read = sem("dve_bank_read")
        high_done = sem("high_done")
        cell_written = sem("cell_written")
        dve_step = sem("dve_step")
        stat_ready = sem("stat_ready")
        var_ready = sem("var_ready")
        root_ready = sem("root_ready")
        rowsum_ready = sem("rowsum_ready")
        split_ready = sem("split_ready")
        dve_shifted = sem("dve_shifted")
        act_shifted = sem("act_shifted")
        dve_entered = sem("dve_entered")
        act_entered = sem("act_entered")
        stored = sem("stored")
        moved = {(b, r, s): sem(f"moved{b}_{r}_{s}") for b in range(HALVES) for r in range(ROWS) for s in range(3)}

        def grid(first):
            return [("cell", i, b) for i in range(first, first + N_GRID) for b in range(HALVES)]

        def both(kind, n):
            return [(kind, n, b) for b in range(HALVES)]

        program = both("norm", 0) + grid(0) + both("norm", 1) + both("conv", N_GRID)
        program += both("norm", 2) + both("gates", 2) + both("norm", 3) + grid(N_GRID + 1)

        jobs, act_count, dve_count, emptied = {}, 0, 0, []
        for st in program:
            n = {"norm": 2, "gates": 1, "conv": 1}.get(st[0]) or banks_of(set_shape(SETS[st[1]])[1])
            jobs[st] = list(range(len(emptied), len(emptied) + n))
            for _ in range(n):
                if st[0] == "cell":
                    act_count += 1
                    emptied.append((act_bank_read, act_count))
                else:
                    dve_count += 1
                    emptied.append((dve_bank_read, dve_count))
        number = {st: len([o for o in program[:program.index(st)] if o[0] == st[0]]) for st in program}
        feeding = [st for st in program if st[0] == "norm" and st[1] != 2]

        def moves(st):
            _, i, b = st
            _, c, r = SETS[i]
            outs = streams_out(c, r)
            tiles = TILES[len(outs)]
            source = cell_out[b][cell_no[st] % 2]
            each = NI // tiles
            found = []
            for g, s in enumerate(outs):
                tc, tr = target(c, r, s)
                if tc == COLS:
                    continue
                together = len(streams_in(tc, tr)) == 3
                for part, quad, plane in places(tc, tr, s)[:1 if together else None]:
                    parts, planes = (slice(0, 2),) * 2 if together else (slice(part, part + 1), slice(plane, plane + 1))
                    for t in range(tiles):
                        for par in range(2):
                            p = 128 // tiles * t + Q * g + C * par
                            d = Q * quad + C * par
                            found.append((moved[b, tr, s], source[p:p + C, 0:each, parts],
                                          inp[b][tr][d:d + C, t * each:t * each + each, planes, par:par + PAIRS]))
            return found

        cells = [st for st in program if st[0] == "cell"]
        cell_no = {st: n // HALVES for n, st in enumerate(cells)}
        totals = {}
        arrivals, left = {}, {}
        for st in cells:
            _, i, b = st
            _, c, r = SETS[i]
            arrivals[st] = [] if (c, r) == (0, 0) else [(moved[b, r, s], totals[b, r, s]) for s in streams_in(c, r)]
            for s in streams_out(c, r):
                tc, tr = target(c, r, s)
                n = len([m for m in moves(st) if m[0] is moved[b, tr, s]]) if tc < COLS else 0
                if n:
                    totals[b, tr, s] = totals.get((b, tr, s), 0) + 16 * n
                    left.setdefault(st, []).append((moved[b, tr, s], totals[b, tr, s]))

        def written(st):
            return emptied[jobs[st][-1]][1]

        block = ctx.enter_context(nc.Block())

        @block.sync
        def _(sp):
            def load_weights(i):
                n_in, n_out = set_shape(SETS[i])
                rows, width = WEIGHT_ROWS[n_in], TAPS * n_out * Q
                if i >= RAW_RING:
                    sp.wait_ge(weights_ready, i - RAW_RING + 1)
                sp.dma_start(raw[0:rows, i % RAW_RING, 0:width], weights[i, 0:rows, 0:width]).then_inc(
                    raw_loaded[i % RAW_RING], 16)

            for b in range(HALVES):
                sp.dma_start(res[:, b, :], x[b]).then_inc(x_loaded[b], 16)
            sp.dma_start(const[:, :], consts).then_inc(consts_loaded, 16)
            sp.dma_start(bias[:, :], biases).then_inc(consts_loaded, 16)
            for i in range(RAW_RING):
                load_weights(i)
            ahead = RAW_RING
            for st in cells:
                sp.wait_ge(cell_written, written(st))
                for signal, source, to in moves(st):
                    sp.dma_start(to, source).then_inc(signal, 16)
                while st[2] == 1 and ahead < len(SETS) and ahead <= st[1] + RAW_RING:
                    load_weights(ahead)
                    ahead += 1
            for b in range(HALVES):
                sp.dma_start(out[b], res[:, b, :]).then_inc(stored, 16)
            sp.wait_ge(stored, 16 * HALVES)

        @block.gpsimd
        def _(pool):
            for b in range(HALVES):
                pool.memset(normed16[b][:, :, :, :], 0.0)
                for r in range(ROWS):
                    pool.memset(inp[b][r][:, :, 0, 0:STORED:PAIRS, :], 0.0)
                    last = pool.memset(inp[b][r][:, :, 1, 0:STORED:PAIRS, :], 0.0)
                for k in range(2):
                    for part in range(2):
                        last = pool.memset(cell_out[b][k][:, :, part, :, 0:PITCH:PITCH - 1], 0.0)
            last.then_inc(zeroed, 1)
            for i, s in enumerate(SETS):
                n_in, n_out = set_shape(s)
                rows, width = WEIGHT_ROWS[n_in], TAPS * n_out * Q
                slot = i % W_RING
                f = raw[0:rows, i % RAW_RING, 0:width]
                pool.wait_ge(raw_loaded[i % RAW_RING], 16 * (i // RAW_RING + 1))
                if i >= W_RING:
                    kind = "conv" if SETS[i - W_RING][0] == "L1" else "cell"
                    pool.wait_ge(sums_ready, jobs[kind, i - W_RING, HALVES - 1][-1] + 1)
                if i:
                    pool.wait_ge(weights_ready, i)
                pool.tensor_scalar(f, f, W_SCALE, None, ALU.mult).then_inc(raw_scaled, 1)
                pool.wait_ge(raw_scaled, i + 1)
                pool.tensor_copy(w16[0:rows, slot, 0, 0:width], f).then_inc(raw_high, 1)
                pool.wait_ge(raw_high, i + 1)
                a, z, plane = {1: (2 * Q, 3 * Q, 0), 2: (0, 2 * Q, 1), 3: (0, 3 * Q, 1)}[n_in]
                pool.tensor_tensor(w16[a:z, slot, plane, 0:width], raw[a:z, i % RAW_RING, 0:width],
                                   w16[a:z, slot, 0, 0:width], ALU.subtract).then_inc(weights_ready, 1)

        @block.tensor
        def _(pe):
            def free_bank(j):
                if j >= BANKS:
                    pe.wait_ge(*emptied[j - BANKS])

            def conv(st):
                _, i, b = st
                n_in, n_out = set_shape(SETS[i])
                m, tiles = n_out * Q, TILES[n_out]
                source = inp[b][0 if st[0] == "conv" else SETS[i][2]]
                steps = [(rows, plane, w_plane, tap) for rows, plane, w_plane in PASSES[n_in] for tap in range(TAPS)]
                for k, j in enumerate(jobs[st]):
                    free_bank(j)
                    for n, (rows, plane, w_plane, tap) in enumerate(steps):
                        dx, off = tap // 2, tap % 2
                        for t in range(tiles):
                            p = 128 // tiles * t
                            last = pe.matmul(bank[j % BANKS][p:p + m, :],
                                             w16[0:rows, i % W_RING, w_plane, tap * m:tap * m + m],
                                             source[0:rows, t * len(jobs[st]) + k, plane, off:off + PAIRS, dx:dx + SIDE],
                                             start=n == 0, stop=n == len(steps) - 1)
                    last.then_inc(sums_ready, 1)

            pe.wait_ge(consts_loaded, 32)
            pe.wait_ge(zeroed, 1)
            for st in program:
                kind, i, b = st
                if kind == "norm":
                    for k, j in enumerate(jobs[st]):
                        free_bank(j)
                        pe.wait_ge(stat_ready, 2 * number[st] + k + 1)
                        pe.matmul(bank[j % BANKS][:, 0:1], averager, stat[:, b, 4 * k:4 * k + 1],
                                  start=True, stop=True).then_inc(sums_ready, 1)
                elif kind == "gates":
                    j = jobs[st][0]
                    free_bank(j)
                    pe.wait_ge(rowsum_ready, number[st] + 1)
                    pe.matmul(bank[j % BANKS][:, 0:SIDE], partner, rowsum[:, b, :],
                              start=True, stop=True).then_inc(sums_ready, 1)
                else:
                    if b == 0:
                        pe.wait_ge(weights_ready, i + 1)
                    if kind == "conv" or SETS[i][1:] == (0, 0):
                        n = feeding.index(("norm", {0: 0, N_GRID: 1, N_GRID + 1: 3}[i], b)) + 1
                        pe.wait_ge(dve_entered, n)
                        pe.wait_ge(act_entered, n)
                    else:
                        for signal, count in arrivals[st]:
                            pe.wait_ge(signal, count)
                    conv(st)

        def enter(eng, copy, st, shares, shifted, entered):
            b, n = st[2], feeding.index(st)
            eng.wait_ge(split_ready, n + 1)
            for part, quad in shares:
                for j in range(NI):
                    last = copy(inp[b][0][Q * quad:Q * quad + Q, j, 0, 1:STORED, :],
                                normed16[b][Q * j:Q * j + Q, part, 0:PAIRS, :])
            last.then_inc(shifted, 1)
            eng.wait_ge(shifted, n + 1)
            for part, quad in shares:
                for j in range(NI):
                    last = copy(inp[b][0][Q * quad:Q * quad + C, j, 0, :, :],
                                normed16[b][Q * j:Q * j + C, part, :, :])
            last.then_inc(entered, 1)

        @block.scalar
        def _(act):
            act.wait_ge(consts_loaded, 32)
            act.wait_ge(zeroed, 1)
            n = 0
            for st in program:
                kind, i, b = st
                if kind == "norm":
                    act.wait_ge(var_ready, number[st] + 1)
                    act.activation(stat[:, b, 6:7], stat[:, b, 5:6], ACT.Sqrt).then_inc(root_ready, 1)
                    if st in feeding:
                        enter(act, act.copy, st, [(0, 2)], act_shifted, act_entered)
                elif kind == "cell":
                    _, c, r = SETS[i]
                    p = 3 * Q if set_shape(SETS[i])[1] == 3 else 128
                    col = (0 if i < N_GRID else N_GRID) + c * ROWS + r
                    for j in jobs[st]:
                        act.wait_ge(sums_ready, j + 1)
                        if n >= T_RING:
                            act.wait_ge(cell_written, n - T_RING + 1)
                        act.activation(act_out[0:p, n % T_RING, :], bank[j % BANKS][0:p, :], ACT.Relu,
                                       bias=bias[0:p, col:col + 1], scale=1.0 / W_SCALE).then_inc(act_bank_read, 1)
                        n += 1

        @block.vector
        def _(dve):
            done = [0]

            def step(ins):
                done[0] += 1
                ins.then_inc(dve_step, 1)
                dve.wait_ge(dve_step, done[0])

            def norm(st):
                _, n, b = st
                s = [stat[:, b, k:k + 1] for k in range(16)]
                mean_job, var_job = jobs[st]
                if n == 0:
                    dve.wait_ge(x_loaded[b], 16)
                step(dve.bn_stats(stat6[:, b, :], res[:, b, :]))
                dve.bn_aggr(stat[:, b, 0:2], stat6[:, b, :]).then_inc(stat_ready, 1)
                dve.wait_ge(sums_ready, mean_job + 1)
                step(dve.tensor_copy(s[3], bank[mean_job % BANKS][:, 0:1]))
                dve.tensor_tensor(s[2], s[0], bank[mean_job % BANKS][:, 0:1], ALU.subtract).then_inc(dve_bank_read, 1)
                dve.wait_ge(dve_bank_read, emptied[mean_job][1])
                dve.scalar_tensor_tensor(s[4], s[2], s[2], s[1], ALU.mult, ALU.add).then_inc(stat_ready, 1)
                dve.wait_ge(sums_ready, var_job + 1)
                dve.tensor_copy(s[11], bank[var_job % BANKS][:, 0:1]).then_inc(dve_bank_read, 1)
                dve.wait_ge(dve_bank_read, emptied[var_job][1])
                dve.tensor_scalar(s[5], s[11], GN_EPS, None, ALU.add).then_inc(var_ready, 1)
                dve.wait_ge(var_ready, number[st] + 1)
                dve.wait_ge(root_ready, number[st] + 1)
                step(dve.reciprocal(s[7], s[6]))
                step(dve.scalar_tensor_tensor(s[8], s[5], s[7], s[6], ALU.mult, ALU.add))
                step(dve.tensor_scalar(s[9], s[8], 0.5, None, ALU.mult))
                step(dve.reciprocal(s[10], s[9]))
                step(dve.tensor_scalar(normed[b][:, :], res[:, b, :], s[3], s[10], ALU.subtract, ALU.mult))

            def split(st):
                b = st[2]
                t = normed[b][:, :].rearrange("p (a x) -> p a x", a=PAIRS)
                high = normed16[b][:, 0, 0:PAIRS, 1:1 + SIDE]
                step(dve.tensor_copy(high, t))
                dve.tensor_tensor(normed16[b][:, 1, 0:PAIRS, 1:1 + SIDE], t, high, ALU.subtract).then_inc(split_ready, 1)

            def conv_add(st):
                b, j = st[2], jobs[st][0]
                y = bank[j % BANKS][:, :].rearrange("p (a x) -> p a x", a=PAIRS)
                r = res[:, b, :].rearrange("p (a x) -> p a x", a=PAIRS)
                dve.wait_ge(sums_ready, j + 1)
                step(dve.scalar_tensor_tensor(r[:, 0:PAIRS - 1, 0:SIDE - 1], y[:, 0:PAIRS - 1, 0:SIDE - 1],
                                              1.0 / W_SCALE, r[:, 0:PAIRS - 1, 0:SIDE - 1], ALU.mult, ALU.add))
                dve.scalar_tensor_tensor(r[:, PAIRS - 1, 0:SIDE - 1], y[:, PAIRS - 1, 0:SIDE - 1], row_mask,
                                         r[:, PAIRS - 1, 0:SIDE - 1], ALU.mult, ALU.add).then_inc(dve_bank_read, 1)
                dve.wait_ge(dve_bank_read, emptied[j][1])

            def gates(st):
                b, j = st[2], jobs[st][0]
                t = normed[b][:, :].rearrange("p (a x) -> p a x", a=PAIRS)
                pr = prod[:, b, :].rearrange("p (a x) -> p a x", a=PAIRS)
                dve.tensor_reduce(rowsum[:, b, :], t.rearrange("p a x -> p x a"), AX.X, ALU.add).then_inc(rowsum_ready, 1)
                dve.wait_ge(sums_ready, j + 1)
                total = bank[j % BANKS][:, 0:SIDE].unsqueeze(1).broadcast_to([128, PAIRS, SIDE])
                dve.tensor_tensor(pr, t, total, ALU.mult).then_inc(dve_bank_read, 1)
                dve.wait_ge(dve_bank_read, emptied[j][1])
                step(dve.tensor_reduce(gate[:, b, :], pr, AX.X, ALU.add))
                dots = gate[:, b, :].unsqueeze(2).broadcast_to([128, PAIRS, SIDE])
                step(dve.scalar_tensor_tensor(pr, dots, 0.0, t, ALU.is_gt, ALU.mult))
                step(dve.tensor_tensor(res[:, b, :], res[:, b, :], prod[:, b, :], ALU.add))

            def cell(st):
                _, i, b = st
                last_cell = SETS[i][1:] == (COLS - 1, ROWS - 1)
                p = 3 * Q if set_shape(SETS[i])[1] == 3 else 128
                n = cell_no[st]
                if n >= 2:
                    for signal, count in left.get(("cell", cells[2 * (n - 2)][1], b), []):
                        dve.wait_ge(signal, count)
                for k, j in enumerate(jobs[st]):
                    m = emptied[j][1] - 1
                    t = act_out[0:p, m % T_RING, :]
                    dve.wait_ge(act_bank_read, m + 1)
                    if last_cell:
                        dve.tensor_tensor(res[:, b, :], res[:, b, :], t, ALU.add).then_inc(cell_written, 1)
                        dve.wait_ge(cell_written, m + 1)
                    else:
                        t = t.rearrange("p (a x) -> p a x", a=PAIRS)
                        high = cell_out[b][n % 2][0:p, k, 0, :, 1:1 + SIDE]
                        low = cell_out[b][n % 2][0:p, k, 1, :, 1:1 + SIDE]
                        dve.tensor_copy(high, t).then_inc(high_done, 1)
                        highs[0] += 1
                        dve.wait_ge(high_done, highs[0])
                        dve.tensor_tensor(low, t, high, ALU.subtract).then_inc(cell_written, 1)

            highs = [0]
            dve.wait_ge(zeroed, 1)
            for st in program:
                if st[0] == "norm":
                    norm(st)
                    if st in feeding:
                        split(st)
                        enter(dve, dve.tensor_copy, st, [(0, 0), (1, 1)], dve_shifted, dve_entered)
                elif st[0] == "gates":
                    gates(st)
                elif st[0] == "conv":
                    conv_add(st)
                else:
                    cell(st)

    return nc


def to_lanes(x):
    v = x.reshape(HALVES, NI, C, PAIRS, 2, SIDE).transpose(0, 1, 4, 2, 3, 5)
    return np.ascontiguousarray(v.reshape(HALVES, 128, PIX))


def from_lanes(v):
    v = v.reshape(HALVES, NI, 2, C, PAIRS, SIDE).transpose(0, 1, 3, 4, 2, 5)
    return np.ascontiguousarray(v.reshape(IMAGES, C, SIDE, SIDE))


def weight_set(w, outs, copies):
    n_in = w.shape[1] // C
    v = np.zeros((n_in, 2, C, 3, 2, len(outs), 2, C), w.dtype)
    for g, o in enumerate(outs):
        part = w[o * C:o * C + C].reshape(C, n_in, C, 3, 3)
        for off in range(2):
            for p_in in range(2):
                for p_out in range(2):
                    ky = 2 * off - p_in - p_out + 1
                    if 0 <= ky < 3:
                        v[:, p_in, :, :, off, g, p_out, :] = part[:, :, :, ky, :].transpose(1, 2, 3, 0)
    v = v.reshape(n_in * Q, TAPS * len(outs) * Q)
    return np.concatenate([v] * copies)


def kernel(x, L0_conv_W, L0_conv_b, L1_conv_K, L3_conv_W, L3_conv_b):
    import concourse.bacc as bacc
    from concourse.bass_utils import run_bass_kernel_spmd

    x, k1 = np.asarray(x), np.asarray(L1_conv_K)
    grids = {"L0": (np.asarray(L0_conv_W), np.asarray(L0_conv_b)), "L3": (np.asarray(L3_conv_W), np.asarray(L3_conv_b))}
    weights = np.zeros((len(SETS), 128, TAPS * 3 * Q), np.float32)
    biases = np.zeros((128, 2 * N_GRID), np.float32)
    for i, (layer, c, r) in enumerate(SETS):
        n_in, n_out = set_shape(SETS[i])
        if layer == "L1":
            w = k1.reshape(C, 3, 3, C).transpose(3, 0, 1, 2)
            outs = [0]
        else:
            outs = streams_out(c, r)
            w = grids[layer][0][c, r][:, :n_in * C]
            lanes = np.stack([grids[layer][1][c, r].reshape(3, C)[o] for o in outs])
            lanes = np.repeat(lanes[:, None], 2, axis=1).reshape(-1)
            lanes = np.tile(lanes, TILES[n_out])
            biases[:len(lanes), (0 if layer == "L0" else N_GRID) + c * ROWS + r] = lanes
        v = weight_set(w, outs, WEIGHT_ROWS[n_in] // (n_in * Q))
        weights[i, :v.shape[0], :v.shape[1]] = v
    lane = np.arange(128)
    image, parity, channel = lane // Q, lane // C % 2, lane % C
    same_image = image[:, None] == image[None, :]
    same_group = same_image & (channel[:, None] // 2 == channel[None, :] // 2)
    partners = same_image & (channel[:, None] % 8 == channel[None, :] % 8) & (channel[:, None] != channel[None, :])
    consts = np.zeros((128, 257), np.float32)
    consts[:, 0:128] = np.where(same_group, 0.25, 0.0)
    consts[:, 128:256] = np.where(partners, 1.0, 0.0)
    consts[:, 256] = np.where(parity == 0, 1.0 / W_SCALE, 0.0)

    arrays = {"x_in": to_lanes(x), "weights_in": weights, "biases_in": biases, "consts_in": consts}
    nc = bacc.Bacc("TRN2", target_bir_lowering=False, num_devices=1)
    args = [nc.dram_tensor(n, a.shape, F32, kind="ExternalInput").ap() for n, a in arrays.items()]
    out = nc.dram_tensor("x_out", (HALVES, 128, PIX), F32, kind="ExternalOutput").ap()
    build(nc, *args, out)
    result = run_bass_kernel_spmd(nc, [arrays], core_ids=[0])
    return from_lanes(result.results[0]["x_out"])
```

```python
from contextlib import ExitStack

import numpy as np

import concourse.bass as bass
from concourse import mybir

F32 = mybir.dt.float32
F16 = mybir.dt.float16
ALU = mybir.AluOpType
ACT = mybir.ActivationFunctionType
AX = mybir.AxisListType

COLS, ROWS = 4, 4
N_GRID = COLS * ROWS
C = 16
RIGHT, UP, DOWN = range(3)
IMAGES, SIDE = 8, 32
HALVES = 2
NI = IMAGES // HALVES
PAIRS = SIDE // 2
PITCH = SIDE + 2
STORED = PAIRS + 1
PIX = PAIRS * SIDE
Q = 2 * C
TAPS = 6
W_SCALE = 256.0
GN_EPS = 1e-05
BANKS = 8
T_RING = 4
W_RING = 6
RAW_RING = 3

COPIED_BY = {
    (0, 0): ("dve", "dve", "act"),
    (0, 1): ("dve", "act", "sp"),
    (0, 2): ("dve", "act", "sp"),
    (3, 0): ("dve", ("act", "act", "dve", "dve")),
    (3, 1): ("dve", ("act", "act", "dve", "dve")),
    (3, 2): ("dve", ("act", "act", "dve", "dve")),
}
ENTRY_SHARE = 3
NOT_PACKED = ((1, 0), (1, 1), (3, 1), (3, 2))
COPIED_COLS = (0, COLS - 1)

ORDER = sorted(((c, r) for c in range(COLS) for r in range(ROWS)), key=lambda cr: (2 * cr[0] + cr[1], cr[0]))


def streams_in(c, r):
    if c == 0:
        return [DOWN]
    return [RIGHT] + [UP] * (r < ROWS - 1) + [DOWN] * (r > 0)


def streams_out(c, r):
    if c == COLS - 1:
        return [RIGHT] if r == ROWS - 1 else [DOWN]
    return [RIGHT] + [UP] * (r > 0) + [DOWN] * (r < ROWS - 1)


def copied(c, r):
    return [DOWN] if c in COPIED_COLS and DOWN in streams_out(c, r) else []


def copied_by(c, r, n, t):
    who = COPIED_BY[c, r][n]
    return who if isinstance(who, str) else who[t]


def target(c, r, stream):
    return {RIGHT: (c + 1, r), UP: (c + 1, r - 1), DOWN: (c, r + 1)}[stream]


ONE, TWO, TWO_PACKED, THREE, THREE_PACKED = range(5)


def scheme(c, r):
    plain = (c, r) in NOT_PACKED
    return {1: ONE, 2: TWO if plain else TWO_PACKED, 3: THREE if plain else THREE_PACKED}[len(streams_in(c, r))]


def places(c, r, stream):
    ins = streams_in(c, r)
    i = ins.index(stream)
    if len(ins) == 1:
        return [(0, 0, 0), (1, 1, 0), (0, 2, 0)]
    if len(ins) == 2:
        return [(0, i, 0), (1, 2 + i, 0)]
    return [(0, i, 0), (1, i, 1)]


def products(how):
    def taps(rows, plane, first):
        return [(rows, plane, tap % 2, tap // 2, first + tap) for tap in range(TAPS)]

    if how == ONE:
        return taps(3 * Q, 0, 0)
    if how == TWO:
        return taps(4 * Q, 0, 0) + taps(2 * Q, 0, TAPS)
    if how == TWO_PACKED:
        return taps(4 * Q, 0, 0) + [(4 * Q, 1, 0, dx, TAPS + dx) for dx in range(3)]
    if how == THREE:
        return taps(3 * Q, 0, 0) + taps(3 * Q, 1, 0) + taps(3 * Q, 0, TAPS)
    return taps(4 * Q, 0, 0) + [(3 * Q, 2, off, 0, 2 * TAPS + off) for off in range(2)] + taps(4 * Q, 1, TAPS)


WEIGHTS = {
    ONE: (3 * Q, TAPS, [(slice(2 * Q, 3 * Q), slice(0, TAPS), slice(0, TAPS))]),
    TWO: (4 * Q, TAPS, [(slice(0, 2 * Q), slice(0, TAPS), slice(TAPS, 2 * TAPS))]),
    TWO_PACKED: (4 * Q, TAPS, [(slice(2 * Q * off, 2 * Q * off + 2 * Q), slice(off, TAPS, 2), slice(TAPS, TAPS + 3))
                               for off in range(2)]),
    THREE: (3 * Q, TAPS, [(slice(0, 3 * Q), slice(0, TAPS), slice(TAPS, 2 * TAPS))]),
    THREE_PACKED: (4 * Q, 2 * TAPS + 2, [(slice(3 * Q, 4 * Q), slice(0, 2 * TAPS), slice(0, 2 * TAPS)),
                                         (slice(0, 3 * Q), slice(2 * TAPS, 2 * TAPS + 2), slice(2 * TAPS, 2 * TAPS + 2))]),
}
BLOCKS = 2 * TAPS + 2
TILES = {1: 4, 2: 2, 3: 1}

PACK_BANK = 0
PACK_FAR = 4
PACK_EARLY = 2


CONV = (-1, -1)
SETS = [("L0", c, r) for c, r in ORDER] + [("L1",) + CONV] + [("L3", c, r) for c, r in ORDER]


def set_shape(s):
    if s[0] == "L1":
        return 1, 1
    return len(streams_in(*s[1:])), len(streams_out(*s[1:]))


def scheme_of(s):
    return ONE if s[0] == "L1" else scheme(*s[1:])


def banks_of(n_out):
    return NI // TILES[n_out]


BUSY_N = 256
GROUPS = {(0, 0): 1, (0, 1): 1, (0, 2): 2}
NORM_BUSY = (10, 0, 10)
CONV_BUSY = (0, 0)
GATES_BUSY = 0
ENTRY_BUSY = (28, 0)
CELL_BUSY = {(3, 2, 0): 14, (3, 2, 1): 2, (3, 3, 0): 2, (3, 3, 1): 10}

BOTH = None


def program_order():
    first, second = ([("cell", i, b) for i in range(n, n + N_GRID) for b in range(HALVES)] for n in (0, N_GRID + 1))
    return ([("norm", 0, BOTH)] + first + [("norm", 1, BOTH)] + [("conv", N_GRID, b) for b in range(HALVES)] +
            [("norm", 2, BOTH), ("gates", 2, BOTH), ("norm", 3, BOTH)] + second)


def jobs_of(st):
    return {"norm": 2, "gates": 1, "conv": 1}.get(st[0]) or banks_of(set_shape(SETS[st[1]])[1])


def build(nc, x, weights, biases, consts, out):
    with ExitStack() as ctx:
        def sb(name, shape, dt):
            return ctx.enter_context(nc.sbuf_tensor(name, shape, dt))

        def sem(name):
            return ctx.enter_context(nc.semaphore(name))

        res = sb("res", [128, HALVES, PIX], F32)
        inp = [[sb(f"inp{b}{r}", [128, NI, 2, STORED, PITCH], F16) for r in range(ROWS)] for b in range(HALVES)]
        cell_out = [[sb(f"cell_out{b}{k}", [128, NI, 2, STORED, PITCH], F16) for k in range(2)] for b in range(HALVES)]
        normed16 = [sb(f"normed16_{b}", [128, 2, STORED, PITCH], F16) for b in range(HALVES)]
        normed = sb("normed", [128, HALVES, PIX], F32)
        zeros = sb("zeros", [128, BUSY_N], F16)
        act_out = sb("act_out", [128, T_RING, PIX], F32)
        raw = sb("raw", [128, RAW_RING, BLOCKS * 3 * Q], F32)
        w16 = sb("w16", [128, W_RING, BLOCKS * 3 * Q], F16)
        shifts = {(b, r): sb(f"shifts{b}{r}", [3 * Q, NI, STORED, SIDE], F16) for b in range(HALVES) for r in range(1, ROWS - 1)}
        bias = sb("bias", [128, 2 * COLS * ROWS], F32)
        const = sb("const", [128, 257], F32)
        averager, partner, row_mask = const[:, 0:128], const[:, 128:256], const[:, 256:257]
        stat6 = sb("stat6", [128, HALVES, 6], F32)
        own = sb("own", [128, HALVES, 2], F32)
        mean, offset, share, var4, root, inverse, better, scale = (
            sb(name, [128, HALVES], F32) for name in
            ("mean", "offset", "share", "var4", "root", "inverse", "better", "scale"))
        rowsum = sb("rowsum", [128, HALVES, SIDE], F32)
        prod = sb("prod", [128, HALVES, PIX], F32)
        gate = sb("gate", [128, HALVES, PAIRS], F32)
        bank = [ctx.enter_context(nc.psum_tensor(f"bank{i}", [128, PIX], F32)) for i in range(BANKS)]

        x_loaded = [sem(f"x_loaded{b}") for b in range(HALVES)]
        consts_loaded = sem("consts_loaded")
        raw_loaded = [sem(f"raw_loaded{i}") for i in range(RAW_RING)]
        raw_scaled = sem("raw_scaled")
        raw_high = sem("raw_high")
        low_step = sem("low_step")
        weights_ready = sem("weights_ready")
        zeroed = sem("zeroed")
        zeros_ready = sem("zeros_ready")
        sums_ready = sem("sums_ready")
        act_bank_read = sem("act_bank_read")
        dve_bank_read = sem("dve_bank_read")
        high_done = sem("high_done")
        cell_written = sem("cell_written")
        dve_step = sem("dve_step")
        stat_ready = sem("stat_ready")
        var_ready = sem("var_ready")
        root_ready = sem("root_ready")
        rowsum_ready = sem("rowsum_ready")
        high_split = sem("high_split")
        low_split = sem("low_split")
        dve_shifted = sem("dve_shifted")
        act_shifted = sem("act_shifted")
        dve_entered = sem("dve_entered")
        act_entered = sem("act_entered")
        stored = sem("stored")
        dve_shift_done = sem("dve_shift_done")
        act_shift_done = sem("act_shift_done")
        packed_early = sem("packed_early")
        packed = sem("packed")
        dve_moved = sem("dve_moved")
        act_moved = sem("act_moved")
        moved = {(b, r, s): sem(f"moved{b}_{r}_{s}") for b in range(HALVES) for r in range(ROWS) for s in range(3)}

        program = program_order()
        order = [(st, k) for st in program for k in range(jobs_of(st))]
        jobs = {st: [j for j, (o, _) in enumerate(order) if o == st] for st in program}
        emptied, counts = {}, {act_bank_read: 0, dve_bank_read: 0}
        for st in program:
            signal = act_bank_read if st[0] == "cell" else dve_bank_read
            for j in jobs[st]:
                counts[signal] += 1
                emptied[j] = (signal, counts[signal])
        norms = [st for st in program if st[0] == "norm"]
        feeds = {0: 0, 1: N_GRID, 3: N_GRID + 1}
        entries = [(i, b) for i in feeds.values() for b in range(HALVES)]
        halves = {b: [st for st in program if st[0] == "cell" and st[2] == b] for b in range(HALVES)}

        def moves(st):
            _, i, b = st
            _, c, r = SETS[i]
            outs = streams_out(c, r)
            tiles = TILES[len(outs)]
            source = cell_out[b][cell_no[st] % 2]
            each = NI // tiles
            found = []
            for s in sorted(outs, reverse=True):
                g = outs.index(s)
                tc, tr = target(c, r, s)
                if tc == COLS:
                    continue
                together = len(streams_in(tc, tr)) == 3
                for n, (part, quad, plane) in enumerate(places(tc, tr, s)[:1 if together else None]):
                    parts, planes = (slice(0, 2),) * 2 if together else (slice(part, part + 1), slice(plane, plane + 1))
                    for t in range(tiles):
                        if s in copied(c, r) and copied_by(c, r, n, t) != "sp":
                            continue
                        for par in range(2):
                            p = 128 // tiles * t + Q * g + C * par
                            d = Q * quad + C * par
                            found.append((moved[b, tr, s], source[p:p + C, 0:each, parts, 0:PAIRS],
                                          inp[b][tr][d:d + C, t * each:t * each + each, planes, par:par + PAIRS]))
            return found

        def copies(st, engine, k):
            _, i, b = st
            _, c, r = SETS[i]
            outs = streams_out(c, r)
            tiles = TILES[len(outs)]
            each = NI // tiles
            source = cell_out[b][cell_no[st] % 2]
            found = []
            for s in copied(c, r):
                tc, tr = target(c, r, s)
                for n, (part, quad, plane) in enumerate(places(tc, tr, s)):
                    for t in range(tiles):
                        if copied_by(c, r, n, t) != engine:
                            continue
                        p = 128 // tiles * t + Q * outs.index(s)
                        first = k + 1 - min(group_of(st), each)
                        to = inp[b][tr][:, t * each + first:t * each + k + 1, plane]
                        found.append(((to[Q * quad:Q * quad + Q, :, 1:STORED], source[p:p + Q, first:k + 1, part, 0:PAIRS]),
                                      (to[Q * quad:Q * quad + C], source[p:p + C, first:k + 1, part])))
            return found

        def group_of(st):
            return GROUPS.get(SETS[st[1]][1:], NI)

        copiers = {"dve": (dve_shift_done, dve_moved), "act": (act_shift_done, act_moved)}
        cells = [st for st in program if st[0] == "cell"]
        cell_no = {st: n for b in range(HALVES) for n, st in enumerate(halves[b])}
        packing = [st for st in cells if scheme(*SETS[st[1]][1:]) in (TWO_PACKED, THREE_PACKED)]
        packed_at = {}
        for st in packing:
            n, (_, c, r) = program.index(st), SETS[st[1]]

            def newest(streams):
                sources = [{RIGHT: (c - 1, r), UP: (c - 1, r + 1), DOWN: (c, r - 1)}[s] for s in streams]
                return max(m for m, o in enumerate(program[:n])
                           if o[0] == "cell" and o[2] == st[2] and SETS[o[1]][1:] in sources)

            ins = streams_in(c, r)
            if len(ins) == 3:
                at = program[max(n - PACK_EARLY, newest(ins[:2]) + 2)]
                packed_at.setdefault((at, 0), []).append(("early", st))
                ins = ins[2:]
            near = newest(ins) > n - PACK_FAR
            at = program[n - (1 if near else 2)]
            soon = DOWN in ins and DOWN in copied(c, r - 1)
            packed_at.setdefault((at, 0 if soon else min(PACK_BANK, len(jobs[at]) - 1) + 1), []).append(("late", st))
        places_of = sorted(packed_at, key=lambda a: (program.index(a[0]), a[1]))
        late = [st for place in places_of for which, st in packed_at[place] if which == "late"]
        early = [st for place in places_of for which, st in packed_at[place] if which == "early"]
        pack_no = {st: n + 1 for n, st in enumerate(late)}
        early_no = {st: n + 1 for n, st in enumerate(early)}
        copying = [st for st in cells if copied(*SETS[st[1]][1:])]
        copied_before = {st: sum(len(jobs[o]) for o in copying[:n]) for n, st in enumerate(copying)}
        totals = {}
        arrivals, left, copied_from = {}, {}, {}
        for st in cells:
            _, i, b = st
            _, c, r = SETS[i]
            if (c, r) != (0, 0):
                for s in streams_in(c, r):
                    arrivals[st, s] = []
                    if r and s in copied(c, r - 1) and s == DOWN:
                        if (b, r, s) in totals:
                            arrivals[st, s].append((moved[b, r, s], totals[b, r, s]))
                        above = next(o for o in halves[b] if SETS[o[1]] == (SETS[i][0], c, r - 1))
                        copied_from[st, s] = above
                        arrivals[st, s] += [(done, copied_before[above] + len(jobs[above])) for _, done in copiers.values()]
                    else:
                        arrivals[st, s].append((moved[b, r, s], totals[b, r, s]))
            for s in streams_out(c, r):
                tc, tr = target(c, r, s)
                n = len([m for m in moves(st) if m[0] is moved[b, tr, s]]) if tc < COLS else 0
                if n:
                    totals[b, tr, s] = totals.get((b, tr, s), 0) + 16 * n
                    left.setdefault(st, []).append((moved[b, tr, s], totals[b, tr, s]))
            if st in copied_before:
                left.setdefault(st, []).extend((done, copied_before[st] + len(jobs[st])) for _, done in copiers.values())

        def written(st):
            return emptied[jobs[st][-1]][1]

        block = ctx.enter_context(nc.Block())

        @block.sync
        def _(sp):
            def load_weights(i):
                rows, blocks, _ = WEIGHTS[scheme_of(SETS[i])]
                width = blocks * set_shape(SETS[i])[1] * Q
                if i >= RAW_RING:
                    sp.wait_ge(weights_ready, i - RAW_RING + 1)
                sp.dma_start(raw[0:rows, i % RAW_RING, 0:width], weights[i, 0:rows, 0:width]).then_inc(
                    raw_loaded[i % RAW_RING], 16)

            for b in range(HALVES):
                sp.dma_start(res[:, b, :], x[b]).then_inc(x_loaded[b], 16)
            sp.dma_start(const[:, :], consts).then_inc(consts_loaded, 16)
            sp.dma_start(bias[:, :], biases).then_inc(consts_loaded, 16)
            for i in range(RAW_RING):
                load_weights(i)
            ahead = RAW_RING
            for st in cells:
                sp.wait_ge(cell_written, written(st))
                for signal, source, to in moves(st):
                    sp.dma_start(to, source).then_inc(signal, 16)
                while st[2] == 0 and ahead < len(SETS) and ahead <= st[1] + RAW_RING:
                    load_weights(ahead)
                    ahead += 1
            for b in range(HALVES):
                sp.dma_start(out[b], res[:, b, :]).then_inc(stored, 16)
            sp.wait_ge(stored, 16 * HALVES)

        @block.gpsimd
        def _(pool):
            pool.memset(zeros[:, :], 0.0).then_inc(zeros_ready, 1)
            for b in range(HALVES):
                last = pool.memset(normed16[b][:, :, :, :], 0.0)
            last.then_inc(zeroed, 1)
            for b in range(HALVES):
                for r in range(ROWS):
                    pool.memset(inp[b][r][:, :, 0, 0:STORED:PAIRS, :], 0.0)
                    last = pool.memset(inp[b][r][:, :, 1, 0:STORED:PAIRS, :], 0.0)
            last.then_inc(zeroed, 1)
            n_lows = 0
            for i, s in enumerate(SETS):
                rows, blocks, lows = WEIGHTS[scheme_of(s)]
                m = set_shape(s)[1] * Q
                width = blocks * m
                slot = i % W_RING
                f = raw[0:rows, i % RAW_RING, 0:width]
                pool.wait_ge(raw_loaded[i % RAW_RING], 16 * (i // RAW_RING + 1))
                if i >= W_RING:
                    kind = "conv" if SETS[i - W_RING][0] == "L1" else "cell"
                    pool.wait_ge(sums_ready, jobs[kind, i - W_RING, HALVES - 1][-1] + 1)
                if i == 1:
                    pool.wait_ge(zeroed, 3)
                if i:
                    pool.wait_ge(weights_ready, i)
                pool.tensor_scalar(f, f, W_SCALE, None, ALU.mult).then_inc(raw_scaled, 1)
                pool.wait_ge(raw_scaled, i + 1)
                pool.tensor_copy(w16[0:rows, slot, 0:width], f).then_inc(raw_high, 1)
                pool.wait_ge(raw_high, i + 1)
                f, w = (v.rearrange("p (k m) -> p k m", m=m) for v in (raw[:, i % RAW_RING, 0:blocks * m],
                                                                       w16[:, slot, 0:BLOCKS * m]))
                for n, (lanes, loaded, to) in enumerate(lows):
                    if n:
                        n_lows += 1
                        low.then_inc(low_step, 1)
                        pool.wait_ge(low_step, n_lows)
                    low = pool.tensor_tensor(w[lanes, to], f[lanes, loaded], w[lanes, loaded], ALU.subtract)
                low.then_inc(weights_ready, 1)
                if i == 0:
                    pool.wait_ge(weights_ready, 1)
                    for b in range(HALVES):
                        for k in range(2):
                            for part in range(2):
                                pool.memset(cell_out[b][k][:, :, part, :, 0:PITCH:PITCH - 1], 0.0)
                                last = pool.memset(cell_out[b][k][:, :, part, PAIRS, 1:1 + SIDE], 0.0)
                    last.then_inc(zeroed, 1)

        @block.tensor
        def _(pe):
            def conv(st, k):
                _, i, b = st
                n_in, n_out = set_shape(SETS[i])
                m, tiles = n_out * Q, TILES[n_out]
                r = 0 if st[0] == "conv" else SETS[i][2]
                steps = products(scheme_of(SETS[i]))
                j = jobs[st][k]
                for n, (rows, plane, off, dx, block_no) in enumerate(steps):
                    if k == 0 and st in pack_no and plane == 1 and steps[n - 1][1] != 1:
                        pe.wait_ge(packed, pack_no[st])
                    for t in range(tiles):
                        p, image = 128 // tiles * t, t * len(jobs[st]) + k
                        source = shifts[b, r][0:rows, image] if plane == 2 else inp[b][r][0:rows, image, plane]
                        last = pe.matmul(bank[j % BANKS][p:p + m, :],
                                         w16[0:rows, i % W_RING, block_no * m:block_no * m + m],
                                         source[:, off:off + PAIRS, dx:dx + SIDE],
                                         start=n == 0, stop=n == len(steps) - 1)
                last.then_inc(sums_ready, 1)

            def still_missing(st, s, k):
                if (st, s) not in copied_from:
                    return 0
                n = len(jobs[copied_from[st, s]])
                group = min(group_of(copied_from[st, s]), n)
                needed = max(image % n for image in range(k, NI, len(jobs[st])))
                return n - group * (needed // group + 1)

            def keep_busy(j, n):
                for _ in range(n):
                    pe.matmul(bank[j % BANKS][:, 0:BUSY_N], zeros[:, 0:128], zeros[:, :], start=True, stop=True)

            pe.wait_ge(zeros_ready, 1)
            for j, (st, k) in enumerate(order):
                kind, i, b = st
                if j >= BANKS:
                    pe.wait_ge(*emptied[j - BANKS])
                if kind == "norm":
                    keep_busy(j, NORM_BUSY[0 if i == 0 else 1 if k == 0 else 2])
                elif kind == "gates":
                    keep_busy(j, GATES_BUSY)
                elif kind == "conv":
                    keep_busy(j, CONV_BUSY[b])
                elif k == 0 and (i, b) in entries:
                    keep_busy(j, ENTRY_BUSY[b])
                elif k == 0:
                    keep_busy(j, CELL_BUSY.get((SETS[i][1], SETS[i][2], b), 0))
                if j == 0:
                    pe.wait_ge(consts_loaded, 32)
                if kind == "norm":
                    pe.wait_ge(stat_ready, 2 * i + k + 1)
                    pe.matmul(bank[j % BANKS][:, 0:HALVES], averager, share[:, :] if k else own[:, :, 0],
                              start=True, stop=True).then_inc(sums_ready, 1)
                elif kind == "gates":
                    pe.wait_ge(rowsum_ready, 1)
                    pe.matmul(bank[j % BANKS][:, 0:HALVES * SIDE], partner, rowsum[:, :, :].rearrange("p b x -> p (b x)"),
                              start=True, stop=True).then_inc(sums_ready, 1)
                else:
                    if k == 0:
                        pe.wait_ge(zeroed, 2)
                        pe.wait_ge(weights_ready, i + 1)
                    if (i, b) not in entries:
                        for s in streams_in(*SETS[i][1:]):
                            for signal, count in arrivals[st, s] if k == 0 or (st, s) in copied_from else []:
                                if signal is not moved[b, SETS[i][2], s]:
                                    count -= still_missing(st, s, k)
                                pe.wait_ge(signal, count)
                        if k == 0:
                            if st in early_no:
                                pe.wait_ge(packed_early, early_no[st])
                    if (i, b) in entries:
                        n = NI * entries.index((i, b)) + TILES[set_shape(SETS[i])[1]] * (k + 1)
                        pe.wait_ge(dve_entered, n)
                        pe.wait_ge(act_entered, n)
                    conv(st, k)

        def enter(eng, copy, i, b, shifted, entered):
            n = entries.index((i, b))
            tiles = TILES[set_shape(SETS[i])[1]]
            images = [t * (NI // tiles) + k for k in range(NI // tiles) for t in range(tiles)]

            def shares(j):
                on_act = images.index(j) < ENTRY_SHARE
                if shifted is act_shifted:
                    return [(0, 2)] * on_act
                return [(0, 0), (1, 1)] + [(0, 2)] * (not on_act)

            for k in range(0, NI, tiles):
                for j in images[k:k + tiles]:
                    for part, quad in shares(j):
                        last = copy(inp[b][0][Q * quad:Q * quad + Q, j, 0, 1:STORED, :],
                                    normed16[b][Q * j:Q * j + Q, part, 0:PAIRS, :])
                last.then_inc(shifted, tiles)
                eng.wait_ge(shifted, NI * n + k + tiles)
                for j in images[k:k + tiles]:
                    for part, quad in shares(j):
                        last = copy(inp[b][0][Q * quad:Q * quad + C, j, 0, :, :],
                                    normed16[b][Q * j:Q * j + C, part, :, :])
                last.then_inc(entered, tiles)

        def copier(eng, copy, name):
            shift_done, done = copiers[name]

            def shift(st, k):
                if st in copied_before and (k + 1) % min(group_of(st), len(jobs[st])) == 0:
                    eng.wait_ge(cell_written, emptied[jobs[st][k]][1])
                    for (to, source), _ in copies(st, name, k):
                        last = copy(to, source)
                    last.then_inc(shift_done, min(group_of(st), len(jobs[st])))

            def even_rows(st, k):
                if st in copied_before and (k + 1) % min(group_of(st), len(jobs[st])) == 0:
                    eng.wait_ge(shift_done, copied_before[st] + k + 1)
                    for _, (to, source) in copies(st, name, k):
                        last = copy(to, source)
                    last.then_inc(done, min(group_of(st), len(jobs[st])))

            return shift, even_rows

        @block.scalar
        def _(act):
            shift, even_rows = copier(act, act.copy, "act")
            act.wait_ge(consts_loaded, 32)
            act.wait_ge(zeroed, 2)
            n = 0
            for st in program:
                kind, i, b = st
                if kind == "norm":
                    act.wait_ge(var_ready, i + 1)
                    act.activation(root[:, :], var4[:, :], ACT.Sqrt).then_inc(root_ready, 1)
                    if i in feeds:
                        for b in range(HALVES):
                            act.wait_ge(high_split, entries.index((feeds[i], b)) + 1)
                            enter(act, act.copy, feeds[i], b, act_shifted, act_entered)
                elif kind == "cell":
                    _, c, r = SETS[i]
                    p = 3 * Q if set_shape(SETS[i])[1] == 3 else 128
                    col = (0 if i < N_GRID else N_GRID) + c * ROWS + r
                    for k, j in enumerate(jobs[st]):
                        act.wait_ge(sums_ready, j + 1)
                        if n >= T_RING:
                            act.wait_ge(cell_written, n - T_RING + 1)
                        act.activation(act_out[0:p, n % T_RING, :], bank[j % BANKS][0:p, :], ACT.Relu,
                                       bias=bias[0:p, col:col + 1], scale=1.0 / W_SCALE).then_inc(act_bank_read, 1)
                        n += 1
                        if k > 1:
                            even_rows(st, k - 2)
                        if k:
                            shift(st, k - 1)
                    if k:
                        even_rows(st, k - 1)
                    shift(st, k)
                    even_rows(st, k)

        @block.vector
        def _(dve):
            done = [0]

            def step(ins):
                done[0] += 1
                ins.then_inc(dve_step, 1)
                dve.wait_ge(dve_step, done[0])

            def norm(st):
                n = st[1]
                mean_job, var_job = jobs[st]
                for b in range(HALVES):
                    if n == 0:
                        dve.wait_ge(x_loaded[b], 16)
                    last = dve.bn_stats(stat6[:, b, :], res[:, b, :])
                step(last)
                for b in range(HALVES):
                    last = dve.bn_aggr(own[:, b, :], stat6[:, b, :])
                last.then_inc(stat_ready, 1)
                dve.wait_ge(sums_ready, mean_job + 1)
                dve.tensor_copy(mean[:, :], bank[mean_job % BANKS][:, 0:HALVES])
                dve.tensor_tensor(offset[:, :], own[:, :, 0], bank[mean_job % BANKS][:, 0:HALVES],
                                  ALU.subtract).then_inc(dve_bank_read, 1)
                dve.wait_ge(dve_bank_read, emptied[mean_job][1])
                for b in range(HALVES):
                    last = dve.scalar_tensor_tensor(share[:, b:b + 1], offset[:, b:b + 1], offset[:, b:b + 1],
                                                    own[:, b, 1:2], ALU.mult, ALU.add)
                last.then_inc(stat_ready, 1)
                dve.wait_ge(sums_ready, var_job + 1)
                dve.tensor_scalar(var4[:, :], bank[var_job % BANKS][:, 0:HALVES], GN_EPS, 0.25,
                                  ALU.add, ALU.mult).then_inc(dve_bank_read, 1)
                dve.wait_ge(dve_bank_read, emptied[var_job][1])
                dve.sem_inc(var_ready, 1)
                dve.wait_ge(root_ready, n + 1)
                step(dve.reciprocal(inverse[:, :], root[:, :]))
                for b in range(HALVES):
                    last = dve.scalar_tensor_tensor(better[:, b:b + 1], var4[:, b:b + 1], inverse[:, b:b + 1],
                                                    root[:, b:b + 1], ALU.mult, ALU.add)
                step(last)
                step(dve.reciprocal(scale[:, :], better[:, :]))
                for b in range(HALVES):
                    ins = dve.tensor_scalar(normed[:, b, :], res[:, b, :], mean[:, b:b + 1], scale[:, b:b + 1],
                                            ALU.subtract, ALU.mult)
                    if n in feeds:
                        step(ins)
                        split(n, b)
                if n not in feeds:
                    step(ins)

            def split(n, b):
                e = entries.index((feeds[n], b)) + 1
                t = normed[:, b, :].rearrange("p (a x) -> p a x", a=PAIRS)
                high = normed16[b][:, 0, 0:PAIRS, 1:1 + SIDE]
                dve.wait_ge(zeroed, 2)
                dve.tensor_copy(high, t).then_inc(high_split, 1)
                dve.wait_ge(high_split, e)
                dve.tensor_tensor(normed16[b][:, 1, 0:PAIRS, 1:1 + SIDE], t, high, ALU.subtract).then_inc(low_split, 1)
                dve.wait_ge(low_split, e)
                enter(dve, dve.tensor_copy, feeds[n], b, dve_shifted, dve_entered)

            def conv_add(st):
                b, j = st[2], jobs[st][0]
                y = bank[j % BANKS][:, :].rearrange("p (a x) -> p a x", a=PAIRS)
                r = res[:, b, :].rearrange("p (a x) -> p a x", a=PAIRS)
                dve.wait_ge(sums_ready, j + 1)
                step(dve.scalar_tensor_tensor(r[:, 0:PAIRS - 1, 0:SIDE - 1], y[:, 0:PAIRS - 1, 0:SIDE - 1],
                                              1.0 / W_SCALE, r[:, 0:PAIRS - 1, 0:SIDE - 1], ALU.mult, ALU.add))
                dve.scalar_tensor_tensor(r[:, PAIRS - 1, 0:SIDE - 1], y[:, PAIRS - 1, 0:SIDE - 1], row_mask,
                                         r[:, PAIRS - 1, 0:SIDE - 1], ALU.mult, ALU.add).then_inc(dve_bank_read, 1)
                dve.wait_ge(dve_bank_read, emptied[j][1])

            def gates(st):
                j = jobs[st][0]
                t, pr = ([v[:, b, :].rearrange("p (a x) -> p a x", a=PAIRS) for b in range(HALVES)]
                         for v in (normed, prod))
                for b in range(HALVES):
                    last = dve.tensor_reduce(rowsum[:, b, :], t[b].rearrange("p a x -> p x a"), AX.X, ALU.add)
                last.then_inc(rowsum_ready, 1)
                dve.wait_ge(sums_ready, j + 1)
                for b in range(HALVES):
                    total = bank[j % BANKS][:, b * SIDE:b * SIDE + SIDE].unsqueeze(1).broadcast_to([128, PAIRS, SIDE])
                    last = dve.tensor_tensor(pr[b], t[b], total, ALU.mult)
                last.then_inc(dve_bank_read, 1)
                dve.wait_ge(dve_bank_read, emptied[j][1])
                for b in range(HALVES):
                    last = dve.tensor_reduce(gate[:, b, :], pr[b], AX.X, ALU.add)
                step(last)
                for b in range(HALVES):
                    dots = gate[:, b, :].unsqueeze(2).broadcast_to([128, PAIRS, SIDE])
                    last = dve.scalar_tensor_tensor(pr[b], dots, 0.0, t[b], ALU.is_gt, ALU.mult)
                step(last)
                for b in range(HALVES):
                    last = dve.tensor_tensor(res[:, b, :], res[:, b, :], prod[:, b, :], ALU.add)
                step(last)

            def pack(at, bank_no):
                for which, st in packed_at.get((at, bank_no), []):
                    _, i, b = st
                    r = SETS[i][2]
                    to = inp[b][r]
                    ins = streams_in(*SETS[i][1:])
                    waits = ins[:2] if which == "early" else ins[-1:] if len(ins) == 3 else ins
                    for s in waits:
                        for signal, count in arrivals[st, s]:
                            dve.wait_ge(signal, count)
                    if which == "early":
                        for dx in range(3):
                            dve.tensor_copy(shifts[b, r][Q * dx:Q * dx + Q], to[0:Q, :, 0, :, dx:dx + SIDE])
                        dve.tensor_copy(to[3 * Q:4 * Q, :, 0], to[Q:2 * Q, :, 0]).then_inc(packed_early, 1)
                    elif len(ins) == 3:
                        dve.tensor_copy(to[3 * Q:4 * Q, :, 1], to[2 * Q:3 * Q, :, 0]).then_inc(packed, 1)
                    else:
                        for off in range(2):
                            last = dve.tensor_copy(to[2 * Q * off:2 * Q * off + 2 * Q, :, 1, 0:PAIRS],
                                                   to[0:2 * Q, :, 0, off:off + PAIRS])
                        last.then_inc(packed, 1)

            def cell(st):
                _, i, b = st
                last_cell = SETS[i][1:] == (COLS - 1, ROWS - 1)
                p = 3 * Q if set_shape(SETS[i])[1] == 3 else 128
                n = cell_no[st]
                if n >= 2:
                    for signal, count in left.get(halves[b][n - 2], []):
                        dve.wait_ge(signal, count)
                if n < 2:
                    dve.wait_ge(zeroed, 3)
                for k, j in enumerate(jobs[st]):
                    pack(st, k)
                    m = emptied[j][1] - 1
                    t = act_out[0:p, m % T_RING, :]
                    dve.wait_ge(act_bank_read, m + 1)
                    if last_cell:
                        dve.tensor_tensor(res[:, b, :], res[:, b, :], t, ALU.add).then_inc(cell_written, 1)
                        dve.wait_ge(cell_written, m + 1)
                    else:
                        t = t.rearrange("p (a x) -> p a x", a=PAIRS)
                        high = cell_out[b][n % 2][0:p, k, 0, 0:PAIRS, 1:1 + SIDE]
                        low = cell_out[b][n % 2][0:p, k, 1, 0:PAIRS, 1:1 + SIDE]
                        dve.tensor_copy(high, t).then_inc(high_done, 1)
                        highs[0] += 1
                        if k:
                            shift(st, k - 1)
                        dve.wait_ge(high_done, highs[0])
                        dve.tensor_tensor(low, t, high, ALU.subtract).then_inc(cell_written, 1)
                    if k:
                        even_rows(st, k - 1)
                shift(st, k)
                pack(st, len(jobs[st]))
                even_rows(st, k)

            highs = [0]
            shift, even_rows = copier(dve, dve.tensor_copy, "dve")
            for st in program:
                if st[0] == "norm":
                    norm(st)
                elif st[0] == "gates":
                    gates(st)
                elif st[0] == "conv":
                    conv_add(st)
                else:
                    cell(st)

    return nc


def to_lanes(x):
    v = x.reshape(HALVES, NI, C, PAIRS, 2, SIDE).transpose(0, 1, 4, 2, 3, 5)
    return np.ascontiguousarray(v.reshape(HALVES, 128, PIX))


def from_lanes(v):
    v = v.reshape(HALVES, NI, 2, C, PAIRS, SIDE).transpose(0, 1, 3, 4, 2, 5)
    return np.ascontiguousarray(v.reshape(IMAGES, C, SIDE, SIDE))


def weight_set(w, outs, how):
    n_in = w.shape[1] // C
    v = np.zeros((n_in, 2, C, 3, 2, len(outs), 2, C), w.dtype)
    for g, o in enumerate(outs):
        part = w[o * C:o * C + C].reshape(C, n_in, C, 3, 3)
        for off in range(2):
            for p_in in range(2):
                for p_out in range(2):
                    ky = 2 * off - p_in - p_out + 1
                    if 0 <= ky < 3:
                        v[:, p_in, :, :, off, g, p_out, :] = part[:, :, :, ky, :].transpose(1, 2, 3, 0)
    m = len(outs) * Q
    v = v.reshape(n_in * Q, TAPS * m)
    if how == THREE_PACKED:
        a = np.concatenate([v, v[Q:2 * Q]])
        b = np.concatenate([v, v[2 * Q:3 * Q]])
        shifts = v[0:Q].reshape(Q, 3, 2 * m).transpose(1, 0, 2).reshape(3 * Q, 2 * m)
        c = np.concatenate([shifts, np.zeros((Q, 2 * m), w.dtype)])
        return np.concatenate([a, b, c], axis=1)
    return np.concatenate([v] * {ONE: 3, TWO: 2, TWO_PACKED: 2, THREE: 1}[how])


def kernel(x, L0_conv_W, L0_conv_b, L1_conv_K, L3_conv_W, L3_conv_b):
    import concourse.bacc as bacc
    from concourse.bass_utils import run_bass_kernel_spmd

    x, k1 = np.asarray(x), np.asarray(L1_conv_K)
    grids = {"L0": (np.asarray(L0_conv_W), np.asarray(L0_conv_b)), "L3": (np.asarray(L3_conv_W), np.asarray(L3_conv_b))}
    weights = np.zeros((len(SETS), 128, BLOCKS * 3 * Q), np.float32)
    biases = np.zeros((128, 2 * N_GRID), np.float32)
    for i, (layer, c, r) in enumerate(SETS):
        n_in, n_out = set_shape(SETS[i])
        if layer == "L1":
            w = k1.reshape(C, 3, 3, C).transpose(3, 0, 1, 2)
            outs = [0]
        else:
            outs = streams_out(c, r)
            w = grids[layer][0][c, r][:, :n_in * C]
            lanes = np.stack([grids[layer][1][c, r].reshape(3, C)[o] for o in outs])
            lanes = np.repeat(lanes[:, None], 2, axis=1).reshape(-1)
            lanes = np.tile(lanes, TILES[n_out])
            biases[:len(lanes), (0 if layer == "L0" else N_GRID) + c * ROWS + r] = lanes
        v = weight_set(w, outs, scheme_of(SETS[i]))
        weights[i, :v.shape[0], :v.shape[1]] = v
    lane = np.arange(128)
    image, parity, channel = lane // Q, lane // C % 2, lane % C
    same_image = image[:, None] == image[None, :]
    same_group = same_image & (channel[:, None] // 2 == channel[None, :] // 2)
    partners = same_image & (channel[:, None] % 8 == channel[None, :] % 8) & (channel[:, None] != channel[None, :])
    consts = np.zeros((128, 257), np.float32)
    consts[:, 0:128] = np.where(same_group, 0.25, 0.0)
    consts[:, 128:256] = np.where(partners, 1.0, 0.0)
    consts[:, 256] = np.where(parity == 0, 1.0 / W_SCALE, 0.0)

    arrays = {"x_in": to_lanes(x), "weights_in": weights, "biases_in": biases, "consts_in": consts}
    nc = bacc.Bacc("TRN2", target_bir_lowering=False, num_devices=1)
    args = [nc.dram_tensor(n, a.shape, F32, kind="ExternalInput").ap() for n, a in arrays.items()]
    out = nc.dram_tensor("x_out", (HALVES, 128, PIX), F32, kind="ExternalOutput").ap()
    build(nc, *args, out)
    result = run_bass_kernel_spmd(nc, [arrays], core_ids=[0])
    return from_lanes(result.results[0]["x_out"])
```

```python
from contextlib import ExitStack

import numpy as np

import concourse.bass as bass
from concourse import mybir

F32 = mybir.dt.float32
F16 = mybir.dt.float16
ALU = mybir.AluOpType
ACT = mybir.ActivationFunctionType
AX = mybir.AxisListType

COLS, ROWS = 4, 4
N_GRID = COLS * ROWS
C = 16
RIGHT, UP, DOWN = range(3)
IMAGES, SIDE = 8, 32
HALVES = 2
NI = IMAGES // HALVES
PAIRS = SIDE // 2
PITCH = SIDE + 2
STORED = PAIRS + 1
PIX = PAIRS * SIDE
Q = 2 * C
TAPS = 6
W_SCALE = 256.0
GN_EPS = 1e-05
BANKS = 8
T_RING = 4
W_RING = 6
RAW_RING = 3

COPIED_COLS = (0, COLS - 1)
COPIED_BY = {
    (0, 0): ("dve", "dve", ("act", "sp")),
    (0, 1): ("dve", "act", "sp"),
    (0, 2): ("dve", "act", "sp"),
    (3, 0): ("dve", ("act", "act", "dve", "dve")),
    (3, 1): ("dve", ("act", "act", "dve", "dve")),
    (3, 2): ("dve", ("act", "act", "dve", "dve")),
}
GROUPS = {(0, 0): 2, (0, 1): 1, (0, 2): 1}
IN_TWO_STEPS = [(0, 1)]
ENTRY_SHARE = 4
HIGH_ON_ACT = [(3, 0), (3, 2)]
NOT_PACKED = [(1, 0), (3, 1), (3, 2)]
SHIFTED_BY_DMA = [(1, 1)]
SETS_BEFORE_SHIFTS = 4
RIGHT_BY_POOL = {(0, 3): 4, (1, 3): 4}
BUSY_N = 256
NORM_BUSY = (0, 8, 2)
GATES_BUSY = 4
CONV_BUSY = (14, 12)
ENTRY_BUSY = (28, 0)
CELL_BUSY = {
    (0, 2, 0): 4, (1, 0, 0): 4, (1, 1, 0): 20, (3, 3, 1): 10,
}

ORDER = sorted(((c, r) for c in range(COLS) for r in range(ROWS)), key=lambda cr: (2 * cr[0] + cr[1], cr[0]))


def streams_in(c, r):
    if c == 0:
        return [DOWN]
    return [RIGHT] + [UP] * (r < ROWS - 1) + [DOWN] * (r > 0)


def streams_out(c, r):
    if c == COLS - 1:
        return [RIGHT] if r == ROWS - 1 else [DOWN]
    return [RIGHT] + [UP] * (r > 0) + [DOWN] * (r < ROWS - 1)


def copied(c, r):
    return [DOWN] if c in COPIED_COLS and DOWN in streams_out(c, r) else []


def copied_by(c, r, n, t):
    who = COPIED_BY[c, r][n]
    return who if isinstance(who, str) else who[t]


def target(c, r, stream):
    return {RIGHT: (c + 1, r), UP: (c + 1, r - 1), DOWN: (c, r + 1)}[stream]


ONE, TWO, TWO_PACKED, THREE, THREE_PACKED = range(5)


def scheme(c, r):
    plain = (c, r) in NOT_PACKED
    return {1: ONE, 2: TWO if plain else TWO_PACKED, 3: THREE if plain else THREE_PACKED}[len(streams_in(c, r))]


def places(c, r, stream):
    ins = streams_in(c, r)
    i = ins.index(stream)
    if len(ins) == 1:
        return [(0, 0, 0), (1, 1, 0), (0, 2, 0)]
    if len(ins) == 2:
        return [(0, i, 0), (1, 2 + i, 0)]
    return [(0, i, 0), (1, i, 1)]


def products(how):
    def taps(rows, plane, first):
        return [(rows, plane, tap % 2, tap // 2, first + tap) for tap in range(TAPS)]

    if how == ONE:
        return taps(3 * Q, 0, 0)
    if how == TWO:
        return taps(4 * Q, 0, 0) + taps(2 * Q, 0, TAPS)
    if how == TWO_PACKED:
        return taps(4 * Q, 0, 0) + [(4 * Q, 1, 0, dx, TAPS + dx) for dx in range(3)]
    if how == THREE:
        return taps(3 * Q, 0, 0) + taps(3 * Q, 1, 0) + taps(3 * Q, 0, TAPS)
    return taps(4 * Q, 0, 0) + [(3 * Q, 2, off, 0, 2 * TAPS + off) for off in range(2)] + taps(4 * Q, 1, TAPS)


WEIGHTS = {
    ONE: (3 * Q, TAPS, [(slice(2 * Q, 3 * Q), slice(0, TAPS), slice(0, TAPS))]),
    TWO: (4 * Q, TAPS, [(slice(0, 2 * Q), slice(0, TAPS), slice(TAPS, 2 * TAPS))]),
    TWO_PACKED: (4 * Q, TAPS, [(slice(2 * Q * off, 2 * Q * off + 2 * Q), slice(off, TAPS, 2), slice(TAPS, TAPS + 3))
                               for off in range(2)]),
    THREE: (3 * Q, TAPS, [(slice(0, 3 * Q), slice(0, TAPS), slice(TAPS, 2 * TAPS))]),
    THREE_PACKED: (4 * Q, 2 * TAPS + 2, [(slice(3 * Q, 4 * Q), slice(0, 2 * TAPS), slice(0, 2 * TAPS)),
                                         (slice(0, 3 * Q), slice(2 * TAPS, 2 * TAPS + 2), slice(2 * TAPS, 2 * TAPS + 2))]),
}
BLOCKS = 2 * TAPS + 2
TILES = {1: 4, 2: 2, 3: 1}

PACK_AHEAD = 2

CONV = (-1, -1)
SETS = [("L0", c, r) for c, r in ORDER] + [("L1",) + CONV] + [("L3", c, r) for c, r in ORDER]


def set_shape(s):
    if s[0] == "L1":
        return 1, 1
    return len(streams_in(*s[1:])), len(streams_out(*s[1:]))


def scheme_of(s):
    return ONE if s[0] == "L1" else scheme(*s[1:])


def banks_of(n_out):
    return NI // TILES[n_out]


BOTH = None

def halves_of(st):
    return range(HALVES) if st[2] is BOTH else [st[2]]


def program_order():
    def grid(first):
        return [("cell", i, b) for i in range(first, first + N_GRID) for b in range(HALVES)]

    def entry(n):
        return [("norm", n, BOTH), ("enter", n, 0), ("enter", n, 1)]

    first, second = grid(0), grid(N_GRID + 1)
    return ([("stats", 0, 0), ("stats", 0, 1)] + entry(0) + first[:-1] + [("stats", 1, 0), first[-1], ("stats", 1, 1)] +
            entry(1) + [("conv", N_GRID, 0), ("stats", 2, 0), ("conv", N_GRID, 1), ("stats", 2, 1)] +
            [("norm", 2, BOTH), ("gates", 2, BOTH)] + entry(3) + second)


def jobs_of(st):
    if st[0] == "cell":
        return banks_of(set_shape(SETS[st[1]])[1])
    return {"norm": 2, "gates": 1, "conv": 1, "stats": 0, "enter": 0}[st[0]]


def build(nc, x, weights, biases, consts, out):
    with ExitStack() as ctx:
        def sb(name, shape, dt):
            return ctx.enter_context(nc.sbuf_tensor(name, shape, dt))

        def sem(name):
            return ctx.enter_context(nc.semaphore(name))

        res = sb("res", [128, HALVES, PIX], F32)
        inp = [[sb(f"inp{b}{r}", [128, NI, 2, STORED, PITCH], F16) for r in range(ROWS)] for b in range(HALVES)]
        cell_out = [[sb(f"cell_out{b}{k}", [128, NI, 2, STORED, PITCH], F16) for k in range(2)] for b in range(HALVES)]
        normed16 = [sb(f"normed16_{b}", [128, 2, STORED, PITCH], F16) for b in range(HALVES)]
        normed = sb("normed", [128, HALVES, PIX], F32)
        zeros = sb("zeros", [128, BUSY_N], F16)
        act_out = sb("act_out", [128, T_RING, PIX], F32)
        raw = sb("raw", [128, RAW_RING, BLOCKS * 3 * Q], F32)
        w16 = sb("w16", [128, W_RING, BLOCKS * 3 * Q], F16)
        shifts = {(b, r): sb(f"shifts{b}{r}", [3 * Q, NI, STORED, PITCH], F16)
                  for b in range(HALVES) for r in range(1, ROWS - 1)}
        bias = sb("bias", [128, 2 * COLS * ROWS], F32)
        const = sb("const", [128, 257], F32)
        averager, partner, row_mask = const[:, 0:128], const[:, 128:256], const[:, 256:257]
        stat6 = sb("stat6", [128, HALVES, 6], F32)
        own = sb("own", [128, HALVES, 2], F32)
        mean, offset, share, var4, root, inverse, better, scale = (
            sb(name, [128, HALVES], F32) for name in
            ("mean", "offset", "share", "var4", "root", "inverse", "better", "scale"))
        rowsum = sb("rowsum", [128, HALVES, SIDE], F32)
        prod = sb("prod", [128, HALVES, PIX], F32)
        gate = sb("gate", [128, HALVES, PAIRS], F32)
        bank = [ctx.enter_context(nc.psum_tensor(f"bank{i}", [128, PIX], F32)) for i in range(BANKS)]

        x_loaded = [sem(f"x_loaded{b}") for b in range(HALVES)]
        consts_loaded = sem("consts_loaded")
        raw_loaded = [sem(f"raw_loaded{i}") for i in range(RAW_RING)]
        raw_scaled = sem("raw_scaled")
        raw_high = sem("raw_high")
        low_step = sem("low_step")
        weights_ready = sem("weights_ready")
        zeroed = sem("zeroed")
        zeros_ready = sem("zeros_ready")
        sums_ready = sem("sums_ready")
        act_bank_read = sem("act_bank_read")
        dve_bank_read = sem("dve_bank_read")
        high_done = sem("high_done")
        cell_written = sem("cell_written")
        dve_step = sem("dve_step")
        stat_ready = sem("stat_ready")
        var_ready = sem("var_ready")
        root_ready = sem("root_ready")
        rowsum_ready = sem("rowsum_ready")
        gated = sem("gated")
        high_split = sem("high_split")
        low_split = sem("low_split")
        dve_shifted = sem("dve_shifted")
        act_shifted = sem("act_shifted")
        dve_entered = sem("dve_entered")
        act_entered = sem("act_entered")
        stored = sem("stored")
        shifts_moved = [sem(f"shifts_moved{b}") for b in range(HALVES)]
        packed_early = sem("packed_early")
        packed = sem("packed")
        dve_shift_done = sem("dve_shift_done")
        act_shift_done = sem("act_shift_done")
        dve_moved = sem("dve_moved")
        act_moved = sem("act_moved")
        moved_early = [sem(f"moved_early{b}") for b in range(HALVES)]
        pool_moved = {(b, r): sem(f"pool_moved{b}_{r}") for b in range(HALVES) for r in {r for _, r in RIGHT_BY_POOL}}
        moved = {(b, r, s): sem(f"moved{b}_{r}_{s}") for b in range(HALVES) for r in range(ROWS) for s in range(3)}

        program = program_order()
        order = [(st, k) for st in program for k in range(jobs_of(st))]
        jobs = {st: [j for j, (o, _) in enumerate(order) if o == st] for st in program}
        emptied, counts = {}, {act_bank_read: 0, dve_bank_read: 0}
        for st in program:
            signal = act_bank_read if st[0] == "cell" else dve_bank_read
            for j in jobs[st]:
                counts[signal] += 1
                emptied[j] = (signal, counts[signal])
        norms = [st for st in program if st[0] == "norm"]
        gatings = [st for st in program if st[0] == "gates"]
        feeds = {0: 0, 1: N_GRID, 3: N_GRID + 1}
        entries = [(feeds[n], b) for kind, n, b in program if kind == "enter"]
        halves = {b: [st for st in program if st[0] == "cell" and st[2] == b] for b in range(HALVES)}

        def arrival(b, r, s, c):
            return pool_moved[b, r] if s == RIGHT and (c, r) in RIGHT_BY_POOL else moved[b, r, s]

        def moves(st, queue="sp"):
            _, i, b = st
            _, c, r = SETS[i]
            outs = streams_out(c, r)
            tiles = TILES[len(outs)]
            source = cell_out[b][cell_no[st] % 2]
            each = NI // tiles
            found = []
            for s in sorted(outs, reverse=True):
                g = outs.index(s)
                tc, tr = target(c, r, s)
                if tc == COLS or (queue == "pool") != (s == RIGHT and (c, r) in RIGHT_BY_POOL):
                    continue
                together = len(streams_in(tc, tr)) == 3
                for n, (part, quad, plane) in enumerate(places(tc, tr, s)[:1 if together else None]):
                    parts, planes = (slice(0, 2),) * 2 if together else (slice(part, part + 1), slice(plane, plane + 1))
                    for t in range(tiles):
                        if s in copied(c, r) and copied_by(c, r, n, t) != "sp":
                            continue
                        steps = [(arrival(b, tr, s, c), 0, each)]
                        if s in copied(c, r) and (c, r) in IN_TWO_STEPS:
                            steps = [(moved_early[b], 0, each // 2), (moved[b, tr, s], each // 2, each)]
                        for signal, first, end in steps:
                            for par in range(2):
                                p = 128 // tiles * t + Q * g + C * par
                                d = Q * quad + C * par
                                found.append((end - 1, signal, source[p:p + C, first:end, parts, 0:PAIRS],
                                              inp[b][tr][d:d + C, t * each + first:t * each + end, planes, par:par + PAIRS]))
            return sorted(found, key=lambda move: move[0])

        def copies(st, engine, k):
            _, i, b = st
            _, c, r = SETS[i]
            outs = streams_out(c, r)
            tiles = TILES[len(outs)]
            each = NI // tiles
            source = cell_out[b][cell_no[st] % 2]
            found = []
            for s in copied(c, r):
                tc, tr = target(c, r, s)
                for n, (part, quad, plane) in enumerate(places(tc, tr, s)):
                    for t in range(tiles):
                        if copied_by(c, r, n, t) != engine:
                            continue
                        p = 128 // tiles * t + Q * outs.index(s)
                        first = k + 1 - min(group_of(st), each)
                        to = inp[b][tr][:, t * each + first:t * each + k + 1, plane]
                        found.append(((to[Q * quad:Q * quad + Q, :, 1:STORED], source[p:p + Q, first:k + 1, part, 0:PAIRS]),
                                      (to[Q * quad:Q * quad + C], source[p:p + C, first:k + 1, part])))
            return found

        def group_of(st):
            return GROUPS.get(SETS[st[1]][1:], NI)

        copiers = {"dve": (dve_shift_done, dve_moved), "act": (act_shift_done, act_moved)}
        cell_no = {st: n for b in range(HALVES) for n, st in enumerate(halves[b])}
        cells = [st for st in program if st[0] == "cell"]
        packing = [st for st in cells if scheme(*SETS[st[1]][1:]) in (TWO_PACKED, THREE_PACKED)]
        packed_at = {}
        for st in packing:
            n, (_, c, r) = cells.index(st), SETS[st[1]]

            def newest(streams):
                sources = [{RIGHT: (c - 1, r), UP: (c - 1, r + 1), DOWN: (c, r - 1)}[s] for s in streams]
                return max(m for m, o in enumerate(cells[:n])
                           if o[2] == st[2] and SETS[o[1]][1:] in sources)

            ins = streams_in(c, r)
            if len(ins) == 3:
                m = newest(ins[:2])
                at = cells[min(n - 1, max(n - PACK_AHEAD, m + 2))]
                packed_at.setdefault((at, len(jobs[at]) + 1 if m == n - 1 else 0), []).append(("early", st))
                ins = ins[2:]
            m = newest(ins)
            at = cells[n - (PACK_AHEAD if m <= n - 2 * HALVES else 1)]
            soon = DOWN in ins and DOWN in copied(c, r - 1)
            bank_no = len(jobs[at]) + 1 if m == n - 1 else 0 if soon else 1
            packed_at.setdefault((at, bank_no), []).append(("late", st))
        places_of = sorted(packed_at, key=lambda a: (program.index(a[0]), a[1]))
        late = [st for place in places_of for which, st in packed_at[place] if which == "late"]
        early = [st for place in places_of for which, st in packed_at[place] if which == "early"]
        pack_no = {st: n + 1 for n, st in enumerate(late)}
        early_no = {st: n + 1 for n, st in enumerate(early)}
        by_dma = [st for st in early if SETS[st[1]][1:] in SHIFTED_BY_DMA]
        shift_no = {st: 16 * 6 * (1 + len([o for o in by_dma[:n] if o[2] == st[2]])) for n, st in enumerate(by_dma)}
        shift_source = {next(o for o in halves[st[2]] if SETS[o[1]] == (SETS[st[1]][0], SETS[st[1]][1] - 1, SETS[st[1]][2])): st
                        for st in by_dma}
        copying = [st for st in cells if copied(*SETS[st[1]][1:])]
        copied_before = {st: sum(len(jobs[o]) for o in copying[:n]) for n, st in enumerate(copying)}
        totals = {}
        arrivals, left, copied_from = {}, {}, {}
        early_total, early_arrival = [0] * HALVES, {}
        for st in cells:
            _, i, b = st
            _, c, r = SETS[i]
            if (c, r) != (0, 0):
                for s in streams_in(c, r):
                    arrivals[st, s] = []
                    if r and s in copied(c, r - 1) and s == DOWN:
                        if moved[b, r, s].name in totals:
                            arrivals[st, s].append((moved[b, r, s], totals[moved[b, r, s].name]))
                        above = next(o for o in halves[b] if SETS[o[1]] == (SETS[i][0], c, r - 1))
                        copied_from[st, s] = above
                        arrivals[st, s] += [(done, copied_before[above] + len(jobs[above])) for _, done in copiers.values()]
                    else:
                        signal = arrival(b, r, s, c - 1)
                        arrivals[st, s].append((signal, totals[signal.name]))
            for s in streams_out(c, r):
                tc, tr = target(c, r, s)
                signal = arrival(b, tr, s, c) if tc < COLS else None
                n = len([m for m in moves(st) + moves(st, "pool") if m[1] is signal])
                if n:
                    totals[signal.name] = totals.get(signal.name, 0) + 16 * n
                    left.setdefault(st, []).append((signal, totals[signal.name]))
            n = len([m for m in moves(st) if m[1] is moved_early[b]])
            if n:
                early_total[b] += 16 * n
                left.setdefault(st, []).append((moved_early[b], early_total[b]))
                early_arrival[b, SETS.index((SETS[i][0], c, r + 1))] = early_total[b]
            if st in shift_source:
                left.setdefault(st, []).append((shifts_moved[b], shift_no[shift_source[st]]))
            if st in copied_before:
                left.setdefault(st, []).extend((done, copied_before[st] + len(jobs[st])) for _, done in copiers.values())

        def written(st):
            return emptied[jobs[st][-1]][1]

        block = ctx.enter_context(nc.Block())

        @block.sync
        def _(sp):
            def load_weights(i):
                rows, blocks, _ = WEIGHTS[scheme_of(SETS[i])]
                width = blocks * set_shape(SETS[i])[1] * Q
                if i >= RAW_RING:
                    sp.wait_ge(weights_ready, i - RAW_RING + 1)
                sp.dma_start(raw[0:rows, i % RAW_RING, 0:width], weights[i, 0:rows, 0:width]).then_inc(
                    raw_loaded[i % RAW_RING], 16)

            for b in range(HALVES):
                sp.dma_start(res[:, b, :], x[b]).then_inc(x_loaded[b], 16)
            sp.dma_start(const[:, :], consts).then_inc(consts_loaded, 16)
            sp.dma_start(bias[:, :], biases).then_inc(consts_loaded, 16)
            for i in range(RAW_RING):
                load_weights(i)
            ahead = RAW_RING
            for st in cells:
                bank_no = -1
                for k, signal, source, to in moves(st):
                    if k > bank_no:
                        sp.wait_ge(cell_written, emptied[jobs[st][k]][1])
                    bank_no = k
                    sp.dma_start(to, source).then_inc(signal, 16)
                if bank_no < len(jobs[st]) - 1:
                    sp.wait_ge(cell_written, written(st))
                while st[2] == 0 and ahead < len(SETS) and ahead <= st[1] + RAW_RING:
                    load_weights(ahead)
                    ahead += 1
            for b in range(HALVES):
                sp.dma_start(out[b], res[:, b, :]).then_inc(stored, 16)
            sp.wait_ge(stored, 16 * HALVES)

        @block.gpsimd
        def _(pool):
            pool.memset(zeros[:, :], 0.0).then_inc(zeros_ready, 1)
            for b in range(HALVES):
                last = pool.memset(normed16[b][:, :, :, :], 0.0)
            last.then_inc(zeroed, 1)
            for b in range(HALVES):
                for r in range(ROWS):
                    pool.memset(inp[b][r][:, :, 0, 0:STORED:PAIRS, :], 0.0)
                    last = pool.memset(inp[b][r][:, :, 1, 0:STORED:PAIRS, :], 0.0)
                    if (b, r) in shifts:
                        last = pool.memset(shifts[b, r][:, :, 0:STORED:PAIRS, :], 0.0)
            last.then_inc(zeroed, 1)
            n_lows = 0
            def move_shifts(st):
                _, i, b = st
                _, c, r = SETS[i]
                pool.wait_ge(cell_written, written(st))
                for dx in range(3):
                    for par in range(2):
                        d = Q * dx + C * par
                        source = cell_out[b][cell_no[st] % 2][C * par:C * par + C, :, 0, 0:PAIRS].rearrange("p i a x -> p i (a x)")
                        to = shifts[b, r][d:d + C, :, par:par + PAIRS].rearrange("p i a x -> p i (a x)")
                        n = PAIRS * PITCH - dx
                        pool.dma_start(to[:, :, 0:n], source[:, :, dx:dx + n]).then_inc(shifts_moved[b], 16)

            for i, s in enumerate(SETS):
                for st in cells:
                    if st[1] + SETS_BEFORE_SHIFTS == i and st in shift_source:
                        move_shifts(st)
                    if st[1] + RIGHT_BY_POOL.get(SETS[st[1]][1:], len(SETS)) == i:
                        pool.wait_ge(cell_written, written(st))
                        for _, signal, source, to in moves(st, "pool"):
                            pool.dma_start(to, source).then_inc(signal, 16)
                rows, blocks, lows = WEIGHTS[scheme_of(s)]
                m = set_shape(s)[1] * Q
                width = blocks * m
                slot = i % W_RING
                f = raw[0:rows, i % RAW_RING, 0:width]
                pool.wait_ge(raw_loaded[i % RAW_RING], 16 * (i // RAW_RING + 1))
                if i >= W_RING:
                    kind = "conv" if SETS[i - W_RING][0] == "L1" else "cell"
                    pool.wait_ge(sums_ready, jobs[kind, i - W_RING, HALVES - 1][-1] + 1)
                if i == 1:
                    pool.wait_ge(zeroed, 3)
                if i:
                    pool.wait_ge(weights_ready, i)
                pool.tensor_scalar(f, f, W_SCALE, None, ALU.mult).then_inc(raw_scaled, 1)
                pool.wait_ge(raw_scaled, i + 1)
                pool.tensor_copy(w16[0:rows, slot, 0:width], f).then_inc(raw_high, 1)
                pool.wait_ge(raw_high, i + 1)
                f, w = (v.rearrange("p (k m) -> p k m", m=m) for v in (raw[:, i % RAW_RING, 0:blocks * m],
                                                                       w16[:, slot, 0:BLOCKS * m]))
                for n, (lanes, loaded, to) in enumerate(lows):
                    if n:
                        n_lows += 1
                        low.then_inc(low_step, 1)
                        pool.wait_ge(low_step, n_lows)
                    low = pool.tensor_tensor(w[lanes, to], f[lanes, loaded], w[lanes, loaded], ALU.subtract)
                low.then_inc(weights_ready, 1)
                if i == 0:
                    pool.wait_ge(weights_ready, 1)
                    for b in range(HALVES):
                        for k in range(2):
                            for part in range(2):
                                pool.memset(cell_out[b][k][:, :, part, :, 0:PITCH:PITCH - 1], 0.0)
                                last = pool.memset(cell_out[b][k][:, :, part, PAIRS, 1:1 + SIDE], 0.0)
                    last.then_inc(zeroed, 1)

        @block.tensor
        def _(pe):
            def conv(st, k):
                _, i, b = st
                n_in, n_out = set_shape(SETS[i])
                m, tiles = n_out * Q, TILES[n_out]
                r = 0 if st[0] == "conv" else SETS[i][2]
                steps = products(scheme_of(SETS[i]))
                j = jobs[st][k]
                for n, (rows, plane, off, dx, block_no) in enumerate(steps):
                    if k == 0 and st in pack_no and plane == 1 and steps[n - 1][1] != 1:
                        pe.wait_ge(packed, pack_no[st])
                    for t in range(tiles):
                        p, image = 128 // tiles * t, t * len(jobs[st]) + k
                        source = shifts[b, r][0:rows, image] if plane == 2 else inp[b][r][0:rows, image, plane]
                        last = pe.matmul(bank[j % BANKS][p:p + m, :],
                                         w16[0:rows, i % W_RING, block_no * m:block_no * m + m],
                                         source[:, off:off + PAIRS, dx:dx + SIDE],
                                         start=n == 0, stop=n == len(steps) - 1)
                last.then_inc(sums_ready, 1)

            def still_missing(st, s, k):
                if (st, s) not in copied_from:
                    return 0
                n = len(jobs[copied_from[st, s]])
                group = min(group_of(copied_from[st, s]), n)
                needed = max(image % n for image in range(k, NI, len(jobs[st])))
                return n - group * (needed // group + 1)

            def early_from(st):
                _, i, b = st
                c, r = SETS[i][1:]
                return i if r and (c, r - 1) in IN_TWO_STEPS else 0

            def keep_busy(j, n):
                for _ in range(n):
                    pe.matmul(bank[j % BANKS][:, 0:BUSY_N], zeros[:, 0:128], zeros[:, :], start=True, stop=True)

            pe.wait_ge(zeros_ready, 1)
            for j, (st, k) in enumerate(order):
                kind, i, b = st
                if j >= BANKS:
                    pe.wait_ge(*emptied[j - BANKS])
                if kind == "norm":
                    keep_busy(j, NORM_BUSY[0 if i == 0 else 1 if k == 0 else 2])
                elif kind == "gates":
                    keep_busy(j, GATES_BUSY)
                elif kind == "conv":
                    keep_busy(j, CONV_BUSY[b])
                elif k == 0 and (i, b) in entries:
                    keep_busy(j, ENTRY_BUSY[b])
                elif k == 0:
                    keep_busy(j, CELL_BUSY.get((SETS[i][1], SETS[i][2], b), 0))
                if j == 0:
                    pe.wait_ge(consts_loaded, 32)
                if kind == "norm":
                    pe.wait_ge(stat_ready, 2 * norms.index(st) + k + 1)
                    h = halves_of(st)
                    pe.matmul(bank[j % BANKS][:, 0:len(h)], averager, (share if k else own[:, :, 0])[:, h[0]:h[-1] + 1],
                              start=True, stop=True).then_inc(sums_ready, 1)
                elif kind == "gates":
                    pe.wait_ge(rowsum_ready, gatings.index(st) + 1)
                    h = halves_of(st)
                    pe.matmul(bank[j % BANKS][:, 0:len(h) * SIDE], partner, rowsum[:, h[0]:h[-1] + 1, :].rearrange("p b x -> p (b x)"),
                              start=True, stop=True).then_inc(sums_ready, 1)
                else:
                    if k == 0:
                        pe.wait_ge(zeroed, 2)
                        pe.wait_ge(weights_ready, i + 1)
                    if (i, b) not in entries:
                        for s in streams_in(*SETS[i][1:]):
                            for signal, count in arrivals[st, s] if k == 0 or (st, s) in copied_from else []:
                                if signal is not moved[b, SETS[i][2], s]:
                                    count -= still_missing(st, s, k)
                                elif early_from(st) and k < len(jobs[st]) // 2:
                                    signal, count = moved_early[b], early_arrival[b, early_from(st)]
                                pe.wait_ge(signal, count)
                        if k == 0:
                            if st in early_no:
                                pe.wait_ge(packed_early, early_no[st])
                            if st in shift_no:
                                pe.wait_ge(shifts_moved[b], shift_no[st])
                    if (i, b) in entries:
                        n = NI * entries.index((i, b)) + TILES[set_shape(SETS[i])[1]] * (k + 1)
                        pe.wait_ge(dve_entered, n)
                        pe.wait_ge(act_entered, n)
                    conv(st, k)

        def enter(eng, copy, i, b, shifted, entered):
            n = entries.index((i, b))
            tiles = TILES[set_shape(SETS[i])[1]]
            images = [t * (NI // tiles) + k for k in range(NI // tiles) for t in range(tiles)]

            def shares(j):
                on_act = images.index(j) < ENTRY_SHARE
                if shifted is act_shifted:
                    return [(0, 2)] * on_act
                return [(0, 0), (1, 1)] + [(0, 2)] * (not on_act)

            for k in range(0, NI, tiles):
                for j in images[k:k + tiles]:
                    for part, quad in shares(j):
                        last = copy(inp[b][0][Q * quad:Q * quad + Q, j, 0, 1:STORED, :],
                                    normed16[b][Q * j:Q * j + Q, part, 0:PAIRS, :])
                last.then_inc(shifted, tiles)
                eng.wait_ge(shifted, NI * n + k + tiles)
                for j in images[k:k + tiles]:
                    for part, quad in shares(j):
                        last = copy(inp[b][0][Q * quad:Q * quad + C, j, 0, :, :],
                                    normed16[b][Q * j:Q * j + C, part, :, :])
                last.then_inc(entered, tiles)

        def copier(eng, copy, name):
            shift_done, done = copiers[name]

            def shift(st, k):
                if st in copied_before and (k + 1) % min(group_of(st), len(jobs[st])) == 0:
                    eng.wait_ge(cell_written, emptied[jobs[st][k]][1])
                    for (to, source), _ in copies(st, name, k):
                        last = copy(to, source)
                    last.then_inc(shift_done, min(group_of(st), len(jobs[st])))

            def even_rows(st, k):
                if st in copied_before and (k + 1) % min(group_of(st), len(jobs[st])) == 0:
                    eng.wait_ge(shift_done, copied_before[st] + k + 1)
                    for _, (to, source) in copies(st, name, k):
                        last = copy(to, source)
                    last.then_inc(done, min(group_of(st), len(jobs[st])))

            return shift, even_rows

        @block.scalar
        def _(act):
            shift, even_rows = copier(act, act.copy, "act")
            act.wait_ge(consts_loaded, 32)
            act.wait_ge(zeroed, 2)
            n = 0
            for st in program:
                kind, i, b = st
                if kind == "norm":
                    act.wait_ge(var_ready, norms.index(st) + 1)
                    h = slice(halves_of(st)[0], halves_of(st)[-1] + 1)
                    act.activation(root[:, h], var4[:, h], ACT.Sqrt).then_inc(root_ready, 1)
                elif kind == "enter":
                    act.wait_ge(high_split, entries.index((feeds[i], b)) + 1)
                    enter(act, act.copy, feeds[i], b, act_shifted, act_entered)
                elif kind == "cell":
                    _, c, r = SETS[i]
                    p = 3 * Q if set_shape(SETS[i])[1] == 3 else 128
                    col = (0 if i < N_GRID else N_GRID) + c * ROWS + r
                    high_too = (c, r) in HIGH_ON_ACT and (c, r) != (COLS - 1, ROWS - 1)
                    if high_too:
                        if cell_no[st] < 2:
                            act.wait_ge(zeroed, 3)
                        else:
                            for signal, count in left.get(halves[b][cell_no[st] - 2], []):
                                act.wait_ge(signal, count)
                    for k, j in enumerate(jobs[st]):
                        act.wait_ge(sums_ready, j + 1)
                        if high_too:
                            act.activation(cell_out[b][cell_no[st] % 2][0:p, k, 0, 0:PAIRS, 1:1 + SIDE],
                                           bank[j % BANKS][0:p, :].rearrange("p (a x) -> p a x", a=PAIRS), ACT.Relu,
                                           bias=bias[0:p, col:col + 1], scale=1.0 / W_SCALE)
                        if n >= T_RING:
                            act.wait_ge(cell_written, n - T_RING + 1)
                        act.activation(act_out[0:p, n % T_RING, :], bank[j % BANKS][0:p, :], ACT.Relu,
                                       bias=bias[0:p, col:col + 1], scale=1.0 / W_SCALE).then_inc(act_bank_read, 1)
                        n += 1
                        if k > 1:
                            even_rows(st, k - 2)
                        if k:
                            shift(st, k - 1)
                    if k:
                        even_rows(st, k - 1)
                    shift(st, k)
                    even_rows(st, k)

        @block.vector
        def _(dve):
            done = [0]

            def step(ins):
                done[0] += 1
                ins.then_inc(dve_step, 1)
                dve.wait_ge(dve_step, done[0])

            last_stats = {}

            def stats(st):
                _, n, b = st
                if n == 0:
                    dve.wait_ge(x_loaded[b], 16)
                last_stats[b] = dve.bn_stats(stat6[:, b, :], res[:, b, :])

            def norm(st):
                n, h = st[1], halves_of(st)
                mean_job, var_job = jobs[st]
                hs = slice(h[0], h[-1] + 1)
                step(last_stats[h[-1]])
                for b in h:
                    last = dve.bn_aggr(own[:, b, :], stat6[:, b, :])
                last.then_inc(stat_ready, 1)
                dve.wait_ge(sums_ready, mean_job + 1)
                dve.tensor_copy(mean[:, hs], bank[mean_job % BANKS][:, 0:len(h)])
                dve.tensor_tensor(offset[:, hs], own[:, hs, 0], bank[mean_job % BANKS][:, 0:len(h)],
                                  ALU.subtract).then_inc(dve_bank_read, 1)
                dve.wait_ge(dve_bank_read, emptied[mean_job][1])
                for b in h:
                    last = dve.scalar_tensor_tensor(share[:, b:b + 1], offset[:, b:b + 1], offset[:, b:b + 1],
                                                    own[:, b, 1:2], ALU.mult, ALU.add)
                last.then_inc(stat_ready, 1)
                dve.wait_ge(sums_ready, var_job + 1)
                dve.tensor_scalar(var4[:, hs], bank[var_job % BANKS][:, 0:len(h)], GN_EPS, 0.25,
                                  ALU.add, ALU.mult).then_inc(dve_bank_read, 1)
                dve.wait_ge(dve_bank_read, emptied[var_job][1])
                dve.sem_inc(var_ready, 1)
                dve.wait_ge(root_ready, norms.index(st) + 1)
                step(dve.reciprocal(inverse[:, hs], root[:, hs]))
                for b in h:
                    last = dve.scalar_tensor_tensor(better[:, b:b + 1], var4[:, b:b + 1], inverse[:, b:b + 1],
                                                    root[:, b:b + 1], ALU.mult, ALU.add)
                step(last)
                step(dve.reciprocal(scale[:, hs], better[:, hs]))
                if n not in feeds:
                    for b in h:
                        ins = normalise(b)
                    step(ins)

            def normalise(b):
                return dve.tensor_scalar(normed[:, b, :], res[:, b, :], mean[:, b:b + 1], scale[:, b:b + 1],
                                         ALU.subtract, ALU.mult)

            def split(n, b):
                step(normalise(b))
                e = entries.index((feeds[n], b)) + 1
                t = normed[:, b, :].rearrange("p (a x) -> p a x", a=PAIRS)
                high = normed16[b][:, 0, 0:PAIRS, 1:1 + SIDE]
                dve.wait_ge(zeroed, 2)
                dve.tensor_copy(high, t).then_inc(high_split, 1)
                dve.wait_ge(high_split, e)
                dve.tensor_tensor(normed16[b][:, 1, 0:PAIRS, 1:1 + SIDE], t, high, ALU.subtract).then_inc(low_split, 1)
                dve.wait_ge(low_split, e)
                enter(dve, dve.tensor_copy, feeds[n], b, dve_shifted, dve_entered)

            def conv_add(st):
                b, j = st[2], jobs[st][0]
                y = bank[j % BANKS][:, :].rearrange("p (a x) -> p a x", a=PAIRS)
                r = res[:, b, :].rearrange("p (a x) -> p a x", a=PAIRS)
                dve.wait_ge(sums_ready, j + 1)
                step(dve.scalar_tensor_tensor(r[:, 0:PAIRS - 1, 0:SIDE - 1], y[:, 0:PAIRS - 1, 0:SIDE - 1],
                                              1.0 / W_SCALE, r[:, 0:PAIRS - 1, 0:SIDE - 1], ALU.mult, ALU.add))
                dve.scalar_tensor_tensor(r[:, PAIRS - 1, 0:SIDE - 1], y[:, PAIRS - 1, 0:SIDE - 1], row_mask,
                                         r[:, PAIRS - 1, 0:SIDE - 1], ALU.mult, ALU.add).then_inc(dve_bank_read, 1)
                dve.wait_ge(dve_bank_read, emptied[j][1])

            def gates(st):
                j, h = jobs[st][0], halves_of(st)
                t, pr = ([v[:, b, :].rearrange("p (a x) -> p a x", a=PAIRS) for b in range(HALVES)]
                         for v in (normed, prod))
                for b in h:
                    last = dve.tensor_reduce(rowsum[:, b, :], t[b].rearrange("p a x -> p x a"), AX.X, ALU.add)
                last.then_inc(rowsum_ready, 1)
                dve.wait_ge(sums_ready, j + 1)
                for b in h:
                    total = bank[j % BANKS][:, (b - h[0]) * SIDE:(b - h[0] + 1) * SIDE].unsqueeze(1).broadcast_to([128, PAIRS, SIDE])
                    last = dve.tensor_tensor(pr[b], t[b], total, ALU.mult)
                last.then_inc(dve_bank_read, 1)
                dve.wait_ge(dve_bank_read, emptied[j][1])
                for b in h:
                    last = dve.tensor_reduce(gate[:, b, :], pr[b], AX.X, ALU.add)
                step(last)
                for b in h:
                    dots = gate[:, b, :].unsqueeze(2).broadcast_to([128, PAIRS, SIDE])
                    last = dve.scalar_tensor_tensor(pr[b], dots, 0.0, t[b], ALU.is_gt, ALU.mult)
                step(last)
                for b in h:
                    dve.tensor_tensor(res[:, b, :], res[:, b, :], prod[:, b, :], ALU.add).then_inc(gated, 1)
                for b in h:
                    dve.wait_ge(gated, b + 1)
                    stats(("stats", 3, b))

            def pack(at, bank_no):
                for which, st in packed_at.get((at, bank_no), []):
                    _, i, b = st
                    r = SETS[i][2]
                    to = inp[b][r]
                    ins = streams_in(*SETS[i][1:])
                    waits = ins[:2] if which == "early" else ins[-1:] if len(ins) == 3 else ins
                    for s in waits:
                        for signal, count in arrivals[st, s]:
                            dve.wait_ge(signal, count)
                    if which == "early":
                        if SETS[i][1:] not in SHIFTED_BY_DMA:
                            for dx in range(3):
                                dve.tensor_copy(shifts[b, r][Q * dx:Q * dx + Q, :, :, 0:SIDE], to[0:Q, :, 0, :, dx:dx + SIDE])
                        dve.tensor_copy(to[3 * Q:4 * Q, :, 0], to[Q:2 * Q, :, 0]).then_inc(packed_early, 1)
                    elif len(ins) == 3:
                        dve.tensor_copy(to[3 * Q:4 * Q, :, 1], to[2 * Q:3 * Q, :, 0]).then_inc(packed, 1)
                    else:
                        for off in range(2):
                            last = dve.tensor_copy(to[2 * Q * off:2 * Q * off + 2 * Q, :, 1, 0:PAIRS],
                                                   to[0:2 * Q, :, 0, off:off + PAIRS])
                        last.then_inc(packed, 1)

            def cell(st):
                _, i, b = st
                last_cell = SETS[i][1:] == (COLS - 1, ROWS - 1)
                p = 3 * Q if set_shape(SETS[i])[1] == 3 else 128
                n = cell_no[st]
                if n >= 2:
                    for signal, count in left.get(halves[b][n - 2], []):
                        dve.wait_ge(signal, count)
                if n < 2:
                    dve.wait_ge(zeroed, 3)
                for k, j in enumerate(jobs[st]):
                    pack(st, k)
                    m = emptied[j][1] - 1
                    t = act_out[0:p, m % T_RING, :]
                    dve.wait_ge(act_bank_read, m + 1)
                    if last_cell:
                        dve.tensor_tensor(res[:, b, :], res[:, b, :], t, ALU.add).then_inc(cell_written, 1)
                        dve.wait_ge(cell_written, m + 1)
                    else:
                        t = t.rearrange("p (a x) -> p a x", a=PAIRS)
                        high = cell_out[b][n % 2][0:p, k, 0, 0:PAIRS, 1:1 + SIDE]
                        low = cell_out[b][n % 2][0:p, k, 1, 0:PAIRS, 1:1 + SIDE]
                        if SETS[i][1:] not in HIGH_ON_ACT:
                            dve.tensor_copy(high, t).then_inc(high_done, 1)
                            highs[0] += 1
                        if k:
                            shift(st, k - 1)
                        if SETS[i][1:] not in HIGH_ON_ACT:
                            dve.wait_ge(high_done, highs[0])
                        dve.tensor_tensor(low, t, high, ALU.subtract).then_inc(cell_written, 1)
                    if k:
                        even_rows(st, k - 1)
                shift(st, k)
                pack(st, len(jobs[st]))
                even_rows(st, k)
                pack(st, len(jobs[st]) + 1)

            highs = [0]
            shift, even_rows = copier(dve, dve.tensor_copy, "dve")
            for st in program:
                if st[0] == "stats":
                    stats(st)
                elif st[0] == "norm":
                    norm(st)
                elif st[0] == "enter":
                    split(st[1], st[2])
                elif st[0] == "gates":
                    gates(st)
                elif st[0] == "conv":
                    conv_add(st)
                else:
                    cell(st)

    return nc


def to_lanes(x):
    v = x.reshape(HALVES, NI, C, PAIRS, 2, SIDE).transpose(0, 1, 4, 2, 3, 5)
    return np.ascontiguousarray(v.reshape(HALVES, 128, PIX))


def from_lanes(v):
    v = v.reshape(HALVES, NI, 2, C, PAIRS, SIDE).transpose(0, 1, 3, 4, 2, 5)
    return np.ascontiguousarray(v.reshape(IMAGES, C, SIDE, SIDE))


def weight_set(w, outs, how):
    n_in = w.shape[1] // C
    v = np.zeros((n_in, 2, C, 3, 2, len(outs), 2, C), w.dtype)
    for g, o in enumerate(outs):
        part = w[o * C:o * C + C].reshape(C, n_in, C, 3, 3)
        for off in range(2):
            for p_in in range(2):
                for p_out in range(2):
                    ky = 2 * off - p_in - p_out + 1
                    if 0 <= ky < 3:
                        v[:, p_in, :, :, off, g, p_out, :] = part[:, :, :, ky, :].transpose(1, 2, 3, 0)
    m = len(outs) * Q
    v = v.reshape(n_in * Q, TAPS * m)
    if how == THREE_PACKED:
        a = np.concatenate([v, v[Q:2 * Q]])
        b = np.concatenate([v, v[2 * Q:3 * Q]])
        shifts = v[0:Q].reshape(Q, 3, 2 * m).transpose(1, 0, 2).reshape(3 * Q, 2 * m)
        c = np.concatenate([shifts, np.zeros((Q, 2 * m), w.dtype)])
        return np.concatenate([a, b, c], axis=1)
    return np.concatenate([v] * {ONE: 3, TWO: 2, TWO_PACKED: 2, THREE: 1}[how])


def kernel(x, L0_conv_W, L0_conv_b, L1_conv_K, L3_conv_W, L3_conv_b):
    import concourse.bacc as bacc
    from concourse.bass_utils import run_bass_kernel_spmd

    x, k1 = np.asarray(x), np.asarray(L1_conv_K)
    grids = {"L0": (np.asarray(L0_conv_W), np.asarray(L0_conv_b)), "L3": (np.asarray(L3_conv_W), np.asarray(L3_conv_b))}
    weights = np.zeros((len(SETS), 128, BLOCKS * 3 * Q), np.float32)
    biases = np.zeros((128, 2 * N_GRID), np.float32)
    for i, (layer, c, r) in enumerate(SETS):
        n_in, n_out = set_shape(SETS[i])
        if layer == "L1":
            w = k1.reshape(C, 3, 3, C).transpose(3, 0, 1, 2)
            outs = [0]
        else:
            outs = streams_out(c, r)
            w = grids[layer][0][c, r][:, :n_in * C]
            lanes = np.stack([grids[layer][1][c, r].reshape(3, C)[o] for o in outs])
            lanes = np.repeat(lanes[:, None], 2, axis=1).reshape(-1)
            lanes = np.tile(lanes, TILES[n_out])
            biases[:len(lanes), (0 if layer == "L0" else N_GRID) + c * ROWS + r] = lanes
        v = weight_set(w, outs, scheme_of(SETS[i]))
        weights[i, :v.shape[0], :v.shape[1]] = v
    lane = np.arange(128)
    image, parity, channel = lane // Q, lane // C % 2, lane % C
    same_image = image[:, None] == image[None, :]
    same_group = same_image & (channel[:, None] // 2 == channel[None, :] // 2)
    partners = same_image & (channel[:, None] % 8 == channel[None, :] % 8) & (channel[:, None] != channel[None, :])
    consts = np.zeros((128, 257), np.float32)
    consts[:, 0:128] = np.where(same_group, 0.25, 0.0)
    consts[:, 128:256] = np.where(partners, 1.0, 0.0)
    consts[:, 256] = np.where(parity == 0, 1.0 / W_SCALE, 0.0)

    arrays = {"x_in": to_lanes(x), "weights_in": weights, "biases_in": biases, "consts_in": consts}
    nc = bacc.Bacc("TRN2", target_bir_lowering=False, num_devices=1)
    args = [nc.dram_tensor(n, a.shape, F32, kind="ExternalInput").ap() for n, a in arrays.items()]
    out = nc.dram_tensor("x_out", (HALVES, 128, PIX), F32, kind="ExternalOutput").ap()
    build(nc, *args, out)
    result = run_bass_kernel_spmd(nc, [arrays], core_ids=[0])
    return from_lanes(result.results[0]["x_out"])
```
